# Optimizing a Trainium2 kernel written in Bass

```python
import numpy as np
import jax
import jax.numpy as jnp

def _softmax(x, axis=-1):
    return jax.nn.softmax(x, axis=axis)

def _gelu(x):
    return jax.nn.gelu(x, approximate=True)

def _silu(x):
    return jax.nn.silu(x)

def _sigmoid(x):
    return jax.nn.sigmoid(x)

def _layernorm(x, axis=-1, eps=1e-05):
    m = jnp.mean(x, axis=axis, keepdims=True)
    v = jnp.var(x, axis=axis, keepdims=True)
    return (x - m) / jnp.sqrt(v + eps)

def _scatter_add(tgt, idx, src, axis=0):
    return tgt.at[idx].add(src)

def _segment_sum(src, seg, n):
    return jax.ops.segment_sum(src, seg, n)
kernel_name = 'mk_decoder_preln_d1_seqx_r4_e8223a'

def setup_inputs(seed: int=0):
    np.random.seed(seed)
    _w = jnp.asarray

    def _rec_inputs():
        import jax
        import jax.numpy as jnp
        _rk = jax.random.key(seed)
        x = 7.22e-05 + 1 * jax.random.normal(jax.random.fold_in(_rk, 1), (8, 512, 256), jnp.float32)
        _lenS = 512 - jax.random.randint(jax.random.fold_in(_rk, 7), (8,), 0, max(1, 512 // 4) + 1, jnp.int32)
        _lenS2 = 512 - jax.random.randint(jax.random.fold_in(_rk, 8), (8,), 0, max(1, 512 // 4) + 1, jnp.int32)
        _ctx_1024P = jax.random.normal(jax.random.fold_in(_rk, 11), (8, 16, 256), jnp.float32)
        _ctx_1024c = jax.random.dirichlet(jax.random.fold_in(_rk, 511), 0.3 * jnp.ones((16,), jnp.float32), (8, 512))
        _ctx_1024t = jnp.einsum('bsk,bkd->bsd', _ctx_1024c, _ctx_1024P)
        _ctx_1024t = _ctx_1024t * jax.lax.rsqrt(jnp.mean(jnp.square(_ctx_1024t)) + 1e-12) * 0.953939
        ctx_1024 = 4.13588e-05 + 0.999923 * (_ctx_1024t + 0.3 * jax.random.normal(jax.random.fold_in(_rk, 611), (8, 512, 256), jnp.float32))
        _validS = jnp.arange(512)[None, :] < _lenS[:, None]
        _validS2 = jnp.arange(512)[None, :] < _lenS2[:, None]
        _causal = jnp.tril(jnp.ones((512, 512), dtype=bool))
        mask_1x1xSxS2_bk0 = jnp.logical_not(jnp.broadcast_to(_validS2[0:1, None, None, :], (1, 1, 512, 512)))
        return (x, ctx_1024, mask_1x1xSxS2_bk0)
    x, ctx_1024, mask_1x1xSxS2_bk0 = _rec_inputs()

    def _L0_attn_setup():
        import jax, jax.numpy as jnp
        import numpy as np
        import math
        B, T, C = (2, 512, 256)
        H, L = (16, 64)
        DH = C // H
        DHE = DH // 2
        THETA = 10000.0

        def _rope_cache(t, dim):
            inv_freq = 1.0 / THETA ** (jnp.arange(0, dim, 2, dtype=jnp.float32) / dim)
            freqs = jnp.arange(t, dtype=jnp.float32)[:, None] * inv_freq[None, :]
            emb = jnp.concatenate((freqs, freqs), axis=-1)
            return (jnp.cos(emb), jnp.sin(emb))

        def _apply_rope(x, cos, sin):
            x1 = x[..., 0::2]
            x2 = x[..., 1::2]
            rot = jnp.stack((-x2, x1), axis=-1).reshape(x.shape)
            return x * cos[None, None] + rot * sin[None, None]
        key = jax.random.key(seed)
        ks = jax.random.split(key, 10)
        s = 0.02
        return {'x': jax.random.normal(ks[0], (B, T, C), jnp.float32), 'Wq_down': jax.random.normal(ks[1], (C, H * L), jnp.float32) * s, 'Wk_down': jax.random.normal(ks[2], (C, H * L), jnp.float32) * s, 'Wv_down': jax.random.normal(ks[3], (C, H * L), jnp.float32) * s, 'Wq_up_c': jax.random.normal(ks[4], (L, DHE), jnp.float32) * s, 'Wq_up_e': jax.random.normal(ks[5], (L, DHE), jnp.float32) * s, 'Wk_up_c': jax.random.normal(ks[6], (L, DHE), jnp.float32) * s, 'Wk_up_e': jax.random.normal(ks[7], (L, DHE), jnp.float32) * s, 'Wv_up': jax.random.normal(ks[8], (L, DH), jnp.float32) * s, 'Wc': jax.random.normal(ks[9], (C, C), jnp.float32) * s}
    _L0_attn_all = _L0_attn_setup()
    _L0_attn_in = {k: v for k, v in _L0_attn_all.items() if k in ('Wq_down', 'Wk_down', 'Wv_down', 'Wq_up_c', 'Wq_up_e', 'Wk_up_c', 'Wk_up_e', 'Wv_up', 'Wc')}
    del _L0_attn_all

    def _L0_xattn_setup():
        import jax, jax.numpy as jnp
        import numpy as np
        B, S, D, H = (4, 512, 256, 16)
        DK = D // H
        key = jax.random.key(seed)
        ks = jax.random.split(key, 11)
        scale = 1.0 / np.sqrt(D)
        inp = {'q': jax.random.normal(ks[0], (B, S, D), dtype=jnp.float32), 'k': jax.random.normal(ks[1], (B, S, D), dtype=jnp.float32), 'v': jax.random.normal(ks[2], (B, S, D), dtype=jnp.float32), 'mask': jnp.tril(jnp.ones((S, S), dtype=bool))[None, None, :, :], 'w_q': jax.random.normal(ks[3], (D, D), dtype=jnp.float32) * scale, 'b_q': jax.random.normal(ks[4], (D,), dtype=jnp.float32) * scale, 'w_k': jax.random.normal(ks[5], (D, D), dtype=jnp.float32) * scale, 'b_k': jax.random.normal(ks[6], (D,), dtype=jnp.float32) * scale, 'w_v': jax.random.normal(ks[7], (D, D), dtype=jnp.float32) * scale, 'b_v': jax.random.normal(ks[8], (D,), dtype=jnp.float32) * scale, 'w_o': jax.random.normal(ks[9], (D, D), dtype=jnp.float32) * scale, 'b_o': jax.random.normal(ks[10], (D,), dtype=jnp.float32) * scale}
        return inp
    _L0_xattn_all = _L0_xattn_setup()
    _L0_xattn_in = {k: v for k, v in _L0_xattn_all.items() if k in ('w_q', 'b_q', 'w_k', 'b_k', 'w_v', 'b_v', 'w_o', 'b_o')}
    del _L0_xattn_all

    def _L0_ffn_setup():
        import jax, jax.numpy as jnp
        import numpy as np
        B, S, HID, DFF, E, K = (4, 512, 256, 1024, 8, 512)
        key = jax.random.key(seed)
        ks = jax.random.split(key, 4)
        sc_h = 1.0 / np.sqrt(HID)
        sc_f = 1.0 / np.sqrt(DFF)
        return {'x': jax.random.normal(ks[0], (B, S, HID), jnp.float32), 'router_w': jax.random.normal(ks[1], (HID, E), jnp.float32) * sc_h, 'router_b': jnp.zeros((E,), jnp.float32), 'w1': jax.random.normal(ks[2], (E, HID, DFF), jnp.float32) * sc_h, 'b1': jnp.zeros((E, DFF), jnp.float32), 'w2': jax.random.normal(ks[3], (E, DFF, HID), jnp.float32) * sc_f, 'b2': jnp.zeros((E, HID), jnp.float32)}
    _L0_ffn_all = _L0_ffn_setup()
    _L0_ffn_in = {k: v for k, v in _L0_ffn_all.items() if k in ('router_w', 'router_b', 'w1', 'b1', 'w2', 'b2')}
    del _L0_ffn_all
    return {'x': x, 'ctx_1024': ctx_1024, 'mask_1x1xSxS2_bk0': mask_1x1xSxS2_bk0, 'L0_attn_Wq_down': _L0_attn_in['Wq_down'], 'L0_attn_Wk_down': _L0_attn_in['Wk_down'], 'L0_attn_Wv_down': _L0_attn_in['Wv_down'], 'L0_attn_Wq_up_c': _L0_attn_in['Wq_up_c'], 'L0_attn_Wq_up_e': _L0_attn_in['Wq_up_e'], 'L0_attn_Wk_up_c': _L0_attn_in['Wk_up_c'], 'L0_attn_Wk_up_e': _L0_attn_in['Wk_up_e'], 'L0_attn_Wv_up': _L0_attn_in['Wv_up'], 'L0_attn_Wc': _L0_attn_in['Wc'], 'L0_xattn_w_q': _L0_xattn_in['w_q'], 'L0_xattn_b_q': _L0_xattn_in['b_q'], 'L0_xattn_w_k': _L0_xattn_in['w_k'], 'L0_xattn_b_k': _L0_xattn_in['b_k'], 'L0_xattn_w_v': _L0_xattn_in['w_v'], 'L0_xattn_b_v': _L0_xattn_in['b_v'], 'L0_xattn_w_o': _L0_xattn_in['w_o'], 'L0_xattn_b_o': _L0_xattn_in['b_o'], 'L0_ffn_router_w': _L0_ffn_in['router_w'], 'L0_ffn_router_b': _L0_ffn_in['router_b'], 'L0_ffn_w1': _L0_ffn_in['w1'], 'L0_ffn_b1': _L0_ffn_in['b1'], 'L0_ffn_w2': _L0_ffn_in['w2'], 'L0_ffn_b2': _L0_ffn_in['b2']}

def reference(x, ctx_1024, mask_1x1xSxS2_bk0, L0_attn_Wq_down, L0_attn_Wk_down, L0_attn_Wv_down, L0_attn_Wq_up_c, L0_attn_Wq_up_e, L0_attn_Wk_up_c, L0_attn_Wk_up_e, L0_attn_Wv_up, L0_attn_Wc, L0_xattn_w_q, L0_xattn_b_q, L0_xattn_w_k, L0_xattn_b_k, L0_xattn_w_v, L0_xattn_b_v, L0_xattn_w_o, L0_xattn_b_o, L0_ffn_router_w, L0_ffn_router_b, L0_ffn_w1, L0_ffn_b1, L0_ffn_w2, L0_ffn_b2):
    import jax
    import jax.numpy as jnp

    def _L0_attn_ref(x, Wq_down, Wk_down, Wv_down, Wq_up_c, Wq_up_e, Wk_up_c, Wk_up_e, Wv_up, Wc):
        import jax, jax.numpy as jnp
        import numpy as np
        import math
        B, T, C = (2, 512, 256)
        H, L = (16, 64)
        DH = C // H
        DHE = DH // 2
        THETA = 10000.0

        def _rope_cache(t, dim):
            inv_freq = 1.0 / THETA ** (jnp.arange(0, dim, 2, dtype=jnp.float32) / dim)
            freqs = jnp.arange(t, dtype=jnp.float32)[:, None] * inv_freq[None, :]
            emb = jnp.concatenate((freqs, freqs), axis=-1)
            return (jnp.cos(emb), jnp.sin(emb))

        def _apply_rope(x, cos, sin):
            x1 = x[..., 0::2]
            x2 = x[..., 1::2]
            rot = jnp.stack((-x2, x1), axis=-1).reshape(x.shape)
            return x * cos[None, None] + rot * sin[None, None]
        b, t, c = x.shape
        q_lat = (x @ Wq_down).reshape(b, t, H, L)
        k_lat = (x @ Wk_down).reshape(b, t, H, L)
        v_lat = (x @ Wv_down).reshape(b, t, H, L)
        q_c = jnp.einsum('bthl,ld->bhtd', q_lat, Wq_up_c)
        q_e = jnp.einsum('bthl,ld->bhtd', q_lat, Wq_up_e)
        k_c = jnp.einsum('bthl,ld->bhtd', k_lat, Wk_up_c)
        k_e = jnp.einsum('bthl,ld->bhtd', k_lat, Wk_up_e)
        v = jnp.einsum('bthl,ld->bhtd', v_lat, Wv_up)
        cos, sin = _rope_cache(t, DHE)
        q = jnp.concatenate([q_c, _apply_rope(q_e, cos, sin)], axis=-1)
        k = jnp.concatenate([k_c, _apply_rope(k_e, cos, sin)], axis=-1)
        scale = 1.0 / math.sqrt(DH)
        scores = jnp.einsum('bhqd,bhkd->bhqk', q, k) * scale
        causal = jnp.tril(jnp.ones((t, t), dtype=bool))
        scores = jnp.where(causal[None, None], scores, -jnp.inf)
        att = jax.nn.softmax(scores, axis=-1)
        y = jnp.einsum('bhqk,bhkd->bhqd', att, v)
        y = y.transpose(0, 2, 1, 3).reshape(b, t, c)
        return y @ Wc

    def _L0_xattn_ref(q, k, v, mask, w_q, b_q, w_k, b_k, w_v, b_v, w_o, b_o):
        import jax, jax.numpy as jnp
        import numpy as np
        B, S, D, H = (4, 512, 256, 16)
        DK = D // H
        b, s, _ = q.shape
        query = q @ w_q.T + b_q
        key_ = k @ w_k.T + b_k
        value = v @ w_v.T + b_v
        query = query.reshape(b, s, H, DK).transpose(0, 2, 1, 3)
        key_ = key_.reshape(b, s, H, DK).transpose(0, 2, 1, 3)
        value = value.reshape(b, s, H, DK).transpose(0, 2, 1, 3)
        scores = jnp.einsum('bhqd,bhkd->bhqk', query, key_) / jnp.sqrt(jnp.asarray(DK, dtype=query.dtype))
        scores = jnp.where(mask, scores, jnp.asarray(-1000000000.0, dtype=scores.dtype))
        attn = jax.nn.softmax(scores, axis=-1)
        x = jnp.einsum('bhqk,bhkd->bhqd', attn, value)
        x = x.transpose(0, 2, 1, 3).reshape(b, s, H * DK)
        return x @ w_o.T + b_o

    def _L0_ffn_ref(x, router_w, router_b, w1, b1, w2, b2):
        import jax, jax.numpy as jnp
        import numpy as np
        B, S, HID, DFF, E, K = (4, 512, 256, 1024, 8, 512)
        b, s, h = x.shape
        xf = x.reshape(-1, h)
        logits = xf @ router_w + router_b
        scores = jax.nn.softmax(logits, axis=-1)
        G, idx = jax.lax.top_k(scores.T, K)
        toks = xf[idx]
        h1 = jax.nn.relu(jnp.einsum('ekh,ehf->ekf', toks, w1) + b1[:, None, :])
        eo = jnp.einsum('ekf,efh->ekh', h1, w2) + b2[:, None, :]
        contrib = (eo * G[..., None]).reshape(-1, h)
        y = jnp.zeros_like(xf).at[idx.reshape(-1)].add(contrib)
        return y.reshape(b, s, h)
    x = x + _L0_attn_ref(_layernorm(x, axis=-1), L0_attn_Wq_down, L0_attn_Wk_down, L0_attn_Wv_down, L0_attn_Wq_up_c, L0_attn_Wq_up_e, L0_attn_Wk_up_c, L0_attn_Wk_up_e, L0_attn_Wv_up, L0_attn_Wc)
    x = x + _L0_xattn_ref(_layernorm(x, axis=-1), ctx_1024, ctx_1024, mask_1x1xSxS2_bk0, L0_xattn_w_q, L0_xattn_b_q, L0_xattn_w_k, L0_xattn_b_k, L0_xattn_w_v, L0_xattn_b_v, L0_xattn_w_o, L0_xattn_b_o)
    x = x + _L0_ffn_ref(_layernorm(x, axis=-1), L0_ffn_router_w, L0_ffn_router_b, L0_ffn_w1, L0_ffn_b1, L0_ffn_w2, L0_ffn_b2)
    return x

_drawn_inputs = setup_inputs


def setup_inputs(seed=0):
    import zlib

    import numpy as np

    out = dict(_drawn_inputs(seed))
    spreads = {'L0_ffn_router_b': (0.0, 2.0), 'L0_ffn_b1': (0.0, 2.0), 'L0_ffn_b2': (0.0, 0.8)}
    factors = {'L0_attn_Wq_down': 8.0,
     'L0_attn_Wk_down': 8.0,
     'L0_attn_Wv_down': 8.0,
     'L0_attn_Wq_up_c': 8.0,
     'L0_attn_Wq_up_e': 8.0,
     'L0_attn_Wk_up_c': 8.0,
     'L0_attn_Wk_up_e': 8.0,
     'L0_attn_Wv_up': 8.0,
     'L0_attn_Wc': 8.0,
     'L0_xattn_b_k': 200.0,
     'L0_xattn_b_q': 21.963,
     'L0_xattn_b_v': 6.751,
     'L0_xattn_b_o': 6.235}
    for name, (base, spread) in spreads.items():
        noise = np.random.default_rng([zlib.crc32(name.encode()), seed]).standard_normal(out[name].shape)
        drawn = base * np.exp(spread * noise) if base else spread * noise
        out[name] = jnp.asarray(drawn.astype(out[name].dtype))
    for name, factor in factors.items():
        out[name] = (out[name] * factor).astype(out[name].dtype)
    return out
```

```python
import concourse.bass as bass
from concourse import mybir
from contextlib import ExitStack

F32 = mybir.dt.float32
F32R = mybir.dt.float32r
BF16 = mybir.dt.bfloat16
I32 = mybir.dt.int32
U8 = mybir.dt.uint8
ALU = mybir.AluOpType
ACT = mybir.ActivationFunctionType
AX = mybir.AxisListType

P = 128
B, S, C = 8, 512, 256
H, DH = 16, 16
LAT = 64
TT = S // P
KT = C // P
GROUPS, GH = 4, 4
TERMS = 3 * DH
MAXROW = 96
STACK = MAXROW + 2
BIG = float(2 ** 30)
EPS = 1e-5
E_N, DFF, CAP = 8, 1024, 512
NT = B * TT
NTOK = B * S
ROW = C + E_N


def plan(part):
    nxt, prev = part != "last", part != "start"

    def p1(i):
        g, n = 1 + i // 16, i % 16
        return [("p1", g, n // TT, n % TT)] + ([("neg", g)] if n == 15 else [])

    proj = [("xt", 0), ("xt", 1), ("qk", 0, 1), ("qk", 0, 0), ("qk", 1, 1), ("qk", 1, 0)]
    if part == "first":
        out = [("ln",)] + proj
        for i in range(48, 64 + AHEAD):
            out += p1(i)
            if i == 65:
                out.append(("mt", 4))
        return out
    extra = {9: [("v", 0)], 15: [("v", 1)], 33: [("og", 0)], 49: [("og", 1)], 50: [("bias",)]}
    extra.update({16 * g + 12: [("mt", g + 1)] for g in range(GROUPS - 1)})
    if nxt:
        extra.update({5: [("ln",)], 16: proj[0:1], 17: proj[1:2], 20: proj[2:3], 22: proj[3:4],
                      24: proj[4:5], 26: proj[5:6], 60: [("mt", 4)]})
    if prev:
        for u, step in ((3, ("og", -2)), (18, ("og", -1)), (27, ("ot", 0, -1)), (28, ("ot", 1, -1)),
                        (30, ("y", 0, -1)), (32, ("y", 1, -1))):
            extra.setdefault(u, []).append(step)
    out = []
    for u in range(16 * GROUPS):
        g, kt, j = u // 16, u // 4 % TT, u % GH
        if g or prev:
            out.append(("pv", g - 1, kt, j))
        out.append(("st", g, kt, j))
        if nxt or u + AHEAD < 48:
            out += p1(u + AHEAD)
        out += extra.get(u, [])
    if part == "last":
        for n in range(16):
            out.append(("pv", 3, n // 4, n % 4))
            if n == 2:
                out.append(("og", 2))
        out += [("og", 3), ("ot", 0, 0), ("ot", 1, 0), ("y", 0, 0), ("y", 1, 0)]
    return out


AHEAD = 5
M_KINDS = ("xt", "qk", "v", "mt", "og", "ot", "y")
FIRST, START, MAIN, LAST = plan("first"), plan("start"), plan("main"), plan("last")


def count(steps, kinds):
    return sum(s[0] in kinds for s in steps)


def before(b, steps_of):
    if b is None:
        return 0
    if isinstance(b, int) and b == 0:
        return steps_of(FIRST)
    return b * steps_of(MAIN) + (steps_of(FIRST) + steps_of(START) - steps_of(MAIN))


assert count(MAIN, M_KINDS) % 2 == 0 and count(MAIN, ("p1",)) % 2 == 0
H_KINDS = ("xt", "qk", "ot")


def m_index(steps, what):
    return count(steps[:steps.index(what)], M_KINDS)


class Turn:

    def __init__(self, b, steps):
        self.b, self.steps = b, steps
        self.m = before(b, lambda s: count(s, M_KINDS))
        self.p1 = before(b, lambda s: count(s, ("p1",)))
        self.st = 0 if b is None else b * (16 * GROUPS)
        self.nxt = 0 if b is None else b + 1
        start = {id(FIRST): [], id(START): FIRST}.get(id(steps), FIRST + START)
        self.m_par = count(start, M_KINDS) % 2
        self.p1_par = count(start, ("p1",)) % 2


def turns(engine, run):
    run(Turn(None, FIRST), FIRST)
    run(Turn(0, START), START)
    with engine.Fori(1, B - 1) as b:
        run(Turn(b, MAIN), MAIN)
    run(Turn(B - 1, LAST), LAST)


def attention_layer(nc, cross, x_in, x_out, dram, ident, identb):
    name = "cross" if cross else "self"
    ctx = ExitStack()
    with ctx:
        def sb(n, shape, dt):
            return ctx.enter_context(nc.sbuf_tensor(f"{name}_{n}", shape, dt))

        def sem(n):
            return ctx.enter_context(nc.semaphore(f"{name}_{n}"))

        xin = sb("xin", [P, TT, C], F32)
        xres = sb("xres", [P, TT, C], F32)
        xn = sb("xn", [P, TT, C], F32)
        stats = sb("stats", [P, TT, 6], F32)
        mv = sb("mv", [P, TT, 2], F32)
        lnw = sb("lnw", [P, 5, TT], F32)
        half_neg = sb("half_neg", [P, TT], F32)
        xt_h = sb("xt_h", [P, KT, S], F32R)
        xt_l = sb("xt_l", [P, KT, S], F32R)
        qk_h = sb("qk_h", [P, 2, 2, S], F32R)
        qk_l = sb("qk_l", [P, 2, 2, S], F32R)
        qst = sb("qst", [P, 2, 8, S], F32R)
        kst = sb("kst", [P, 2, 8, S], F32R)
        probs = sb("probs", [P, TT, GH, S], F32)
        vals = sb("vals", [P, TT, H, 32], F32)
        wqk = sb("wqk", [P, 2, 2, KT, C], F32R)
        wv = sb("wv", [P, 2, KT, C], F32R)
        wo = sb("wo", [P, 2, KT, C], F32R)
        mx = sb("mx", [P, 2, 16], F32)
        neg = sb("neg", [P, 2, 16], F32R)
        shift = sb("shift", [32, P], F32R)
        ones = sb("ones", [P, P], BF16)
        oraw = sb("oraw", [P, 2, S], F32)
        ocomp = sb("ocomp", [P, TT, C], F32)
        rec = sb("rec", [P, 2, 16], F32)
        ot_h = sb("ot_h", [P, KT, S], F32R)
        ot_l = sb("ot_l", [P, KT, S], F32R)
        if cross:
            craw = sb("craw", [P, KT, S], F32)
            ct_h = sb("ct_h", [P, KT, S], F32R)
            ct_l = sb("ct_l", [P, KT, S], F32R)
            lower = sb("lower", [P, TT, S], F32)
            lower_t = sb("lower_t", [P, TT, S], BF16)
            some_key = sb("some_key", [P, S], F32)
            bqk = sb("bqk", [P, 2, 2], F32)
            bv = sb("bv", [P, C], F32)
            bo = sb("bo", [P, C], F32)
            qtmp = sb("qtmp", [P, S], F32)
        else:
            cosb = sb("cosb", [P, S], F32)
            sinb = sb("sinb", [P, S], F32)
            rope_a = sb("rope_a", [P, S], F32)
            rope_b = sb("rope_b", [P, S], F32)
            lower = sb("lower", [P, S], F32)
            lower_t = sb("lower_t", [P, P], BF16)
            up = sb("up", [P, 3, 32], F32)
        room = probs[:, :, :, :].rearrange("p a b c -> p (a b c)")

        ps_p1 = ctx.enter_context(nc.psum_tensor(f"{name}_ps_p1", [P, 2, S], F32))
        ps_st = ctx.enter_context(nc.psum_tensor(f"{name}_ps_st", [P, 2, S], F32))
        ps_o = ctx.enter_context(nc.psum_tensor(f"{name}_ps_o", [P, 2, S], F32))
        ps_m = ctx.enter_context(nc.psum_tensor(f"{name}_ps_m", [P, 2, S], F32))

        held = sem("held")
        w_loaded = sem("w_loaded")
        consts = sem("consts")
        prep_mm = sem("prep_mm")
        prep_act = sem("prep_act")
        prep_dve = sem("prep_dve")
        x_loaded = sem("x_loaded")
        xres_loaded = sem("xres_loaded")
        c_loaded = sem("c_loaded")
        stats_ready = sem("stats_ready")
        pool_chain = sem("pool_chain")
        dve_chain = sem("dve_chain")
        xn_ready = sem("xn_ready")
        ct_split = sem("ct_split")
        m_ready = sem("m_ready")
        m_free = sem("m_free")
        h_done = sem("h_done")
        q_pool = sem("q_pool")
        p1_ready = sem("p1_ready")
        max_done = sem("max_done")
        neg_ready = sem("neg_ready")
        shifted = sem("shifted")
        st_ready = sem("st_ready")
        exp_done = sem("exp_done")
        pv_done = sem("pv_done")
        o_raw = sem("o_raw")
        stacked = [sem("stacked0"), sem("stacked1")]
        res_bias = sem("res_bias")
        stored = sem("stored")
        STACK_DMAS = 12
        POOL_TILES = 2

        x_in_v = x_in.rearrange("(b t p) c -> b p t c", b=B, p=P)
        x_out_v = x_out.rearrange("(b t p) c -> b p t c", b=B, p=P)

        def width(kt):
            return 0 if cross else kt * P

        def keys_of(qt):
            return S if cross else (qt + 1) * P

        block = ctx.enter_context(nc.Block())

        @block.sync
        def _(sp):
            n_w = 0
            if cross:
                for i, k in enumerate(("w_q", "w_k", "w_v", "w_o")):
                    sp.dma_start(room[:, i * KT * C:(i + 1) * KT * C].rearrange("p (a c) -> p a c", a=KT),
                                 dram[k].rearrange("(a p) c -> p a c", p=P)).then_inc(w_loaded, 16)
                sp.dma_start(room[:, 2048:2560].bitcast(U8).rearrange("p (a c) -> p a c", a=TT),
                             dram["mask"].rearrange("(a p) c -> p a c", p=P)).then_inc(w_loaded, 16)
                sp.dma_start(room[:, 2560:3072].bitcast(U8).rearrange("p (a c) -> p a c", a=TT),
                             dram["mask_t"].rearrange("(a p) c -> p a c", p=P)).then_inc(w_loaded, 16)
                sp.dma_start(bqk[:, :, :], dram["b_qk"]).then_inc(w_loaded, 16)
                sp.dma_start(bv[:, :], dram["b_v"].partition_broadcast(P)).then_inc(w_loaded, 16)
                sp.dma_start(bo[:, :], dram["b_o"].partition_broadcast(P)).then_inc(w_loaded, 16)
                sp.dma_start(craw[:, :, :], dram["ctx_t"][0].rearrange("(a p) s -> p a s", p=P)).then_inc(c_loaded, 16)
            else:
                for i in range(3):
                    sp.dma_start(room[:, i * 2048:(i + 1) * 2048].rearrange("p (a c) -> p a c", a=8),
                                 dram["down_t"][i].rearrange("(a p) c -> p a c", p=P)).then_inc(w_loaded, 16)
                sp.dma_start(room[:, 6144:6656].rearrange("p (a c) -> p a c", a=KT),
                             dram["wc"].rearrange("(a p) c -> p a c", p=P)).then_inc(w_loaded, 16)
                sp.dma_start(cosb[:, :], dram["cos"]).then_inc(w_loaded, 16)
                sp.dma_start(sinb[:, :], dram["sin"]).then_inc(w_loaded, 16)
                sp.wait_ge(consts, 1)
                for hh in range(2):
                    for i, (k, lo, n) in enumerate((("q_c", 0, 8), ("q_e", 8, 8), ("k_c", 0, 8), ("k_e", 8, 8), ("v_up", 0, 16))):
                        side = (0, 0, 1, 1, 2)[i]
                        sp.dma_start(up[hh * LAT:(hh + 1) * LAT, side, hh * DH + lo:hh * DH + lo + n],
                                     dram[k]).then_inc(w_loaded, 16)

            def stack(half):
                src = slice(half * 64, half * 64 + 64)
                for dst, side, parts in ((qst, 0, (qk_h, qk_h, qk_l)), (kst, 1, (qk_h, qk_l, qk_h))):
                    for term, part in enumerate(parts):
                        for t in range(2):
                            row = term * DH + t * 8
                            sp.dma_start(dst[row:row + 8, half, :, :].bitcast(F32),
                                         part[src, side, t, :].bitcast(F32)).then_inc(stacked[half], 16)

            sp.wait_ge(consts, 2)
            sp.wait_ge(m_free, 6)
            sp.wait_ge(q_pool, POOL_TILES)
            stack(0)
            stack(1)

            def turn(t, steps):
                b, nxt, prev = t.b, steps is not LAST, steps is not START
                if nxt:
                    if cross:
                        sp.wait_ge(ct_split, b + 1)
                        sp.sem_inc(held, 1)
                        sp.dma_start(craw[:, :, :], dram["ctx_t"][b + 1].rearrange("(a p) s -> p a s", p=P)).then_inc(c_loaded, 16)
                    sp.wait_ge(m_free, t.m + (m_index(steps, ("qk", 1, 0)) + 1))
                    sp.sem_inc(held, 1)
                    sp.wait_ge(q_pool, b * POOL_TILES + 2 * POOL_TILES)
                    sp.sem_inc(held, 1)
                    sp.wait_ge(st_ready, t.st + 2 * 16)
                    sp.sem_inc(held, 1)
                    stack(0)
                if prev:
                    sp.wait_ge(m_free, t.m + (m_index(steps, ("y", 1, -1)) + 1))
                    sp.sem_inc(held, 1)
                    sp.dma_start(x_out_v[b - 1], xres[:, :, :]).then_inc(stored, 16)
                    sp.wait_ge(stored, b * 16)
                    sp.sem_inc(held, 1)
                sp.dma_start(xres[:, :, :], x_in_v[b]).then_inc(xres_loaded, 16)
                if nxt:
                    sp.wait_ge(st_ready, t.st + 4 * 16)
                    sp.sem_inc(held, 1)
                    stack(1)
                else:
                    sp.wait_ge(m_free, t.m + count(steps, M_KINDS))
                    sp.dma_start(x_out_v[b], xres[:, :, :]).then_inc(stored, 16)
                    sp.wait_ge(stored, B * 16)

            turn(Turn(0, START), START)
            with sp.Fori(1, B - 1) as b:
                turn(Turn(b, MAIN), MAIN)
            turn(Turn(B - 1, LAST), LAST)

        @block.gpsimd
        def _(pool):
            nc.gpsimd.dma_start(xin[:, :, :], x_in_v[0]).then_inc(x_loaded, 16)
            n = [0]

            def fill(*ops):
                for op in ops:
                    n[0] += 1
                    op().then_inc(pool_chain, 1)
                    pool.wait_ge(pool_chain, n[0])

            if not cross:
                fill(lambda: nc.gpsimd.memset(up[:, :, :], 0.0))
                pool.sem_inc(consts, 1)
                fill(lambda: nc.gpsimd.memset(lower[:, :], 0.0),
                     lambda: nc.gpsimd.affine_select(out=lower[:, S - P:S], in_=lower[:, S - P:S], compare_op=ALU.is_ge,
                                                     fill=-BIG, base=0, pattern=[[-1, P]], channel_multiplier=1),
                     lambda: nc.gpsimd.memset(lower_t[:, :], 0.0),
                     lambda: nc.gpsimd.affine_select(out=lower_t[:, :], in_=lower_t[:, :], compare_op=ALU.is_ge,
                                                     fill=-BIG, base=0, pattern=[[1, P]], channel_multiplier=-1))
            else:
                pool.sem_inc(consts, 1)
            fill(lambda: nc.gpsimd.memset(half_neg[:, :], -0.5),
                 lambda: nc.gpsimd.memset(vals[:, :, :, :], 0.0),
                 lambda: nc.gpsimd.memset(vals[:, :, :, DH:DH + 1], 1.0))
            pool.wait_ge(prep_dve, 1)
            pool.sem_inc(consts, 1)
            CHAIN0 = n[0]

            def layernorm(chain):
                v, y, a, m = (lnw[:, i, :] for i in range(4))
                seq = (
                    lambda: nc.gpsimd.tensor_scalar(out=v, in0=mv[:, :, 1], scalar1=1.0, scalar2=EPS, op0=ALU.mult, op1=ALU.add),
                    lambda: nc.gpsimd.tensor_tensor(out=y, in0=v, in1=half_neg[:, :], op=ALU.pow),
                    lambda: nc.gpsimd.tensor_tensor(out=a, in0=y, in1=y, op=ALU.mult),
                    lambda: nc.gpsimd.tensor_tensor(out=a, in0=a, in1=v, op=ALU.mult),
                    lambda: nc.gpsimd.tensor_scalar(out=a, in0=a, scalar1=-0.5, scalar2=1.5, op0=ALU.mult, op1=ALU.add),
                    lambda: nc.gpsimd.tensor_tensor(out=y, in0=y, in1=a, op=ALU.mult),
                    lambda: nc.gpsimd.tensor_tensor(out=m, in0=mv[:, :, 0], in1=y, op=ALU.mult),
                    lambda: nc.gpsimd.tensor_scalar(out=m, in0=m, scalar1=-1.0, scalar2=0.0, op0=ALU.mult, op1=ALU.add),
                )
                for i, op in enumerate(seq):
                    op().then_inc(pool_chain, 1)
                    pool.wait_ge(pool_chain, chain + (i + 1))
                    pool.sem_inc(held, 1)
                for t in range(TT):
                    last = nc.gpsimd.tensor_scalar(out=xn[:, t, :], in0=xin[:, t, :], scalar1=y[:, t:t + 1],
                                                   scalar2=m[:, t:t + 1], op0=ALU.mult, op1=ALU.add)
                last.then_inc(xn_ready, 1)

            LN_CHAIN = 8
            CHAIN_TURN = LN_CHAIN + (1 + 2 if cross else 2 * 3)

            def split_context(chain):
                nc.gpsimd.tensor_scalar(out=ct_h[:, :, :], in0=craw[:, :, :], scalar1=1.0, scalar2=0.0,
                                        op0=ALU.mult, op1=ALU.add).then_inc(pool_chain, 1)
                pool.wait_ge(pool_chain, chain + 1)
                nc.gpsimd.tensor_tensor(out=ct_l[:, :, :], in0=craw[:, :, :], in1=ct_h[:, :, :].bitcast(F32),
                                        op=ALU.subtract).then_inc(ct_split, 1)

            def finish_tile(side, t, chain):
                if cross:
                    src = qtmp[:, :]
                    done = 0
                else:
                    nc.gpsimd.tensor_tensor(out=rope_b[:, :], in0=rope_b[:, :], in1=sinb[:, :], op=ALU.mult).then_inc(pool_chain, 1)
                    pool.wait_ge(pool_chain, chain + 1)
                    nc.gpsimd.tensor_tensor(out=rope_a[:, :], in0=rope_a[:, :], in1=rope_b[:, :], op=ALU.add).then_inc(pool_chain, 1)
                    pool.wait_ge(pool_chain, chain + 2)
                    pool.sem_inc(held, 1)
                    src = rope_a[:, :]
                    done = 2
                nc.gpsimd.tensor_scalar(out=qk_h[:, side, t, :], in0=src, scalar1=1.0, scalar2=0.0,
                                        op0=ALU.mult, op1=ALU.add).then_inc(pool_chain, 1)
                pool.wait_ge(pool_chain, chain + (done + 1))
                nc.gpsimd.tensor_tensor(out=qk_l[:, side, t, :], in0=src, in1=qk_h[:, side, t, :].bitcast(F32),
                                        op=ALU.subtract).then_inc(q_pool, 1)
                return done + 1

            def run(t, steps):
                chain, done = CHAIN0 if t.b is None else t.b * CHAIN_TURN + (CHAIN0 + CHAIN_TURN), 0
                if steps is START or steps is MAIN:
                    pool.wait_ge(xn_ready, t.b + 1)
                    pool.sem_inc(held, 1)
                    nc.gpsimd.dma_start(xin[:, :, :], x_in_v[t.b + 1]).then_inc(x_loaded, 16)
                for s in steps:
                    if s[0] == "ln":
                        pool.wait_ge(stats_ready, t.nxt + 1)
                        if t.b is not None:
                            pool.wait_ge(m_ready, t.m)
                        pool.sem_inc(held, 1)
                        layernorm(chain + done)
                        done += LN_CHAIN
                    if s == ("xt", 0) and cross:
                        pool.wait_ge(c_loaded, t.nxt * 16 + 16)
                        if t.b is not None:
                            pool.wait_ge(m_ready, t.m + (m_index(steps, ("v", 1)) + 1))
                        pool.sem_inc(held, 1)
                        split_context(chain + done)
                        done += 1
                    if s[0] == "qk" and (s[1] == 0 if cross else s[2] == 1):
                        pool.wait_ge(m_free, t.m + (m_index(steps, s) + 1))
                        if t.b is not None:
                            pool.wait_ge(stacked[0], t.nxt * (16 * STACK_DMAS))
                            pool.wait_ge(stacked[1], t.nxt * (16 * STACK_DMAS))
                        pool.sem_inc(held, 1)
                        done += finish_tile(s[1], s[2], chain + done)
                    if s[0] == "mt":
                        pool.wait_ge(m_free, t.m + (m_index(steps, s) + 1))
                        pool.sem_inc(held, 1)
                        g = s[1] % GROUPS
                        nc.gpsimd.dma_start(qst[MAXROW:MAXROW + 2, g // 2, (g % 2) * GH:(g % 2 + 1) * GH, :].bitcast(F32),
                                            shift[:, :].bitcast(F32)).then_inc(shifted, 16)
                    if s[0] == "bias" and cross:
                        pool.wait_ge(xres_loaded, t.b * 16 + 16)
                        pool.sem_inc(held, 1)
                        for tt in range(TT):
                            last = nc.gpsimd.tensor_tensor(out=xres[:, tt, :], in0=xres[:, tt, :], in1=bo[:, :], op=ALU.add)
                        last.then_inc(res_bias, 1)
                assert done == (0 if steps is LAST else CHAIN_TURN)

            if cross:
                pool.wait_ge(w_loaded, 16 * 9)
            turns(pool, run)

        @block.tensor
        def _(pe):
            if not cross:
                pe.wait_ge(w_loaded, 16 * 16)
                for i, bank in enumerate((ps_p1[:, 0, :], ps_p1[:, 1, :], ps_st[:, 0, :])):
                    for ct in range(KT):
                        for pair in range(8):
                            at = ct * C + pair * 32
                            last = nc.tensor.matmul(bank[:, at:at + 32],
                                                    room[:, i * 2048 + pair * C + ct * P:i * 2048 + pair * C + ct * P + P],
                                                    up[:, i, :], start=True, stop=True)
                    last.then_inc(prep_mm, 1)
            else:
                pe.wait_ge(prep_dve, 2)
                for kt in range(TT):
                    last = nc.tensor.matmul(ps_p1[:, 0, :], ones[:, :], lower_t[:, kt, :], start=(kt == 0), stop=(kt == TT - 1))
                last.then_inc(prep_mm, 1)

            def three(out, w, wsl, x_h, x_l, xsl, x_first):
                n = 0
                for kt in range(KT):
                    for wp, xp in ((0, x_h), (0, x_l), (1, x_h)):
                        a, c = w(wp, kt)[:, wsl], xp[:, kt, xsl]
                        last = nc.tensor.matmul(out, c if x_first else a, a if x_first else c,
                                                start=(n == 0), stop=(n == 3 * KT - 1))
                        n += 1
                return last

            def run(t, steps):
                m, p1, st = 0, 0, 0
                for s in steps:
                    kind = s[0]
                    if kind in M_KINDS:
                        bank = ps_m[:, (t.m_par + m) % 2, :]
                        if not (t.b is None and m < 2):
                            pe.wait_ge(m_free, t.m + (m - 1))
                    if kind == "xt":
                        if s[1] == 0:
                            pe.wait_ge(xn_ready, t.nxt + 1)
                        for tt in range(TT):
                            last = nc.tensor.transpose(bank[:, tt * P:(tt + 1) * P], xn[:, tt, s[1] * P:(s[1] + 1) * P], ident[:, :])
                    elif kind == "qk":
                        side, tile = s[1:]
                        if (side, tile) == (0, 1):
                            pe.wait_ge(m_free, t.m + (m_index(steps, ("xt", 1)) + 1))
                        if cross and (side, tile) == (1, 1):
                            pe.wait_ge(ct_split, t.nxt + 1)
                        src_h, src_l = (ct_h, ct_l) if cross and side else (xt_h, xt_l)
                        last = three(bank, lambda p, k: wqk[:, p, side, k, :], slice(tile * P, (tile + 1) * P),
                                     src_h, src_l, slice(0, S), False)
                    elif kind == "v":
                        src_h, src_l = (ct_h, ct_l) if cross else (xt_h, xt_l)
                        for i in range(2):
                            tt = 2 * s[1] + i
                            last = three(bank[:, i * C:(i + 1) * C], lambda p, k: wv[:, p, k, :], slice(0, C),
                                         src_h, src_l, slice(tt * P, (tt + 1) * P), True)
                    elif kind == "p1":
                        g, j, qt = s[1] % GROUPS, s[2], s[3]
                        if g % 2 == 0 and j == 0 and qt == 0:
                            batch = t.nxt if s[1] >= GROUPS else t.b
                            pe.wait_ge(stacked[g // 2], batch * (16 * STACK_DMAS) + 16 * STACK_DMAS)
                        if not (t.b is None and p1 < 2):
                            pe.wait_ge(max_done, t.p1 + (p1 - 1))
                        hh = (g % 2) * GH + j
                        last = nc.tensor.matmul(ps_p1[:, (t.p1_par + p1) % 2, 0:keys_of(qt)],
                                                qst[0:MAXROW, g // 2, hh, qt * P:(qt + 1) * P],
                                                kst[0:MAXROW, g // 2, hh, 0:keys_of(qt)], start=True, stop=True)
                        last.then_inc(p1_ready, 1)
                        p1 += 1
                    elif kind == "mt":
                        k = s[1] if t.b is not None else 0
                        pe.wait_ge(neg_ready, (0 if t.b is None else t.b * GROUPS) + (k + 1))
                        last = nc.tensor.transpose(bank[0:32, 0:P], neg[:, :, :].rearrange("p a b -> p (a b)").bitcast(F32), ident[:, :])
                    elif kind == "st":
                        g, kt, j = s[1:]
                        if kt == 0 and j == 0:
                            pe.wait_ge(shifted, t.b * (16 * GROUPS) + 16 * (g + 1))
                        pe.wait_ge(exp_done, t.st + (st + 1))
                        hh = (g % 2) * GH + j
                        lo = width(kt)
                        out = ps_st[:, st % 2, 0:S - lo]
                        last = nc.tensor.matmul(out, kst[0:STACK, g // 2, hh, kt * P:(kt + 1) * P],
                                                qst[0:STACK, g // 2, hh, lo:S], start=True, stop=False)
                        if cross:
                            last = nc.tensor.matmul(out, identb[:, :], lower_t[:, kt, :], start=False, stop=True)
                        else:
                            last = nc.tensor.matmul(ps_st[:, st % 2, 0:P], identb[:, :], lower_t[:, :], start=False, stop=True)
                        last.then_inc(st_ready, 1)
                        st += 1
                    elif kind == "pv":
                        g, kt, j = s[1:]
                        lo = width(kt)
                        if g == 0 and j == 0 and kt % 2 == 0:
                            pe.wait_ge(m_free, t.m + (m_index(steps, ("v", kt // 2)) + 1))
                        if kt == 0 and j == 0:
                            pe.wait_ge(o_raw, t.b * GROUPS + (g + 1))
                        if j == 0:
                            pe.wait_ge(exp_done, t.st + (16 * g + 4 * kt + 4 + 2))
                        last = nc.tensor.matmul(ps_o[32 * j:32 * j + 32, g % 2, lo:S], vals[:, kt, GH * (g % GROUPS) + j, :],
                                                probs[:, kt, j, 0:S - lo], start=(kt == 0), stop=(kt == TT - 1))
                        if kt == TT - 1 and j == GH - 1:
                            last.then_inc(pv_done, 1)
                    elif kind == "og":
                        g = s[1]
                        pe.wait_ge(o_raw, t.b * GROUPS + (g + 3))
                        for qt in range(TT):
                            last = nc.tensor.transpose(bank[:, qt * P:(qt + 1) * P], oraw[:, g % 2, qt * P:(qt + 1) * P], ident[:, :])
                    elif kind == "ot":
                        pe.wait_ge(m_free, t.m + (m_index(steps, ("og", 3 + 4 * s[2])) + 1))
                        for qt in range(TT):
                            last = nc.tensor.transpose(bank[:, qt * P:(qt + 1) * P], ocomp[:, qt, s[1] * P:(s[1] + 1) * P], ident[:, :])
                    elif kind == "y":
                        pe.wait_ge(m_free, t.m + (m_index(steps, ("ot", 1, s[2])) + 1))
                        for i in range(2):
                            tt = 2 * s[1] + i
                            last = three(bank[:, i * C:(i + 1) * C], lambda p, k: wo[:, p, k, :], slice(0, C),
                                         ot_h, ot_l, slice(tt * P, (tt + 1) * P), True)
                    if kind in M_KINDS:
                        last.then_inc(m_ready, 1)
                        m += 1

            pe.wait_ge(prep_dve, 4)
            pe.wait_ge(prep_act, 1)
            pe.wait_ge(consts, 2)
            turns(pe, run)

        def head_order(m, tile):
            return m.rearrange("p (t m d j) -> p t m j d", t=2, m=2, d=8)[:, tile, :, :, :]

        @block.scalar
        def _(act):
            act.sem_inc(exp_done, 2)
            act.sem_inc(o_raw, 2)
            if cross:
                act.wait_ge(w_loaded, 16 * 9)
                for i, dst in enumerate((wqk[:, 0, 0], wqk[:, 0, 1], wv[:, 0], wo[:, 0])):
                    last = nc.scalar.activation(dst, room[:, i * 512:(i + 1) * 512].rearrange("p (a c) -> p a c", a=KT), ACT.Copy)
            else:
                act.wait_ge(prep_mm, 3)
                for side in range(2):
                    for ct in range(KT):
                        for tile in range(2):
                            src = ps_p1[:, side, ct * C:(ct + 1) * C].rearrange("p (m j t d) -> p t m j d", m=2, j=8, t=2)[:, tile]
                            nc.scalar.activation(head_order(wqk[:, 0, side, ct, :], tile), src, ACT.Copy)
                nc.scalar.activation(wv[:, 0, :, :], ps_st[:, 0, :].rearrange("p (a c) -> p a c", a=KT), ACT.Copy)
                act.wait_ge(w_loaded, 16 * 16)
                last = nc.scalar.activation(wo[:, 0, :, :], room[:, 6144:6656].rearrange("p (a c) -> p a c", a=KT), ACT.Copy)
            last.then_inc(prep_act, 1)
            act.wait_ge(prep_dve, 4)
            act.wait_ge(consts, 2)

            def run(t, steps):
                m, st, hd = 0, 0, 0
                for s in steps:
                    kind = s[0]
                    if kind in H_KINDS and not (kind == "qk" and (s[1] == 0 if cross else s[2] == 1)):
                        bank = ps_m[:, (t.m_par + m) % 2, :]
                        act.wait_ge(m_ready, t.m + (m + 1))
                        if kind == "xt":
                            nc.scalar.activation(xt_h[:, s[1], :], bank, ACT.Copy).then_inc(h_done, 1)
                        elif kind == "ot":
                            nc.scalar.activation(ot_h[:, s[1], :], bank, ACT.Copy).then_inc(h_done, 1)
                        else:
                            if t.b is not None:
                                act.wait_ge(stacked[0], t.nxt * (16 * STACK_DMAS))
                                act.wait_ge(stacked[1], t.nxt * (16 * STACK_DMAS))
                            if cross:
                                nc.scalar.activation(qk_h[:, s[1], s[2], :], bank, ACT.Identity, bias=bqk[:, s[1], s[2]:s[2] + 1]).then_inc(h_done, 1)
                            else:
                                nc.scalar.activation(qk_h[:, s[1], s[2], :], bank, ACT.Copy).then_inc(h_done, 1)
                    if kind in M_KINDS:
                        m += 1
                    if kind == "st":
                        g, kt, j = s[1:]
                        n = S - width(kt)
                        act.wait_ge(st_ready, t.st + (st + 1))
                        nc.scalar.activation(probs[:, kt, j, 0:n], ps_st[:, st % 2, 0:n], ACT.Exp,
                                             scale=float(DH) ** -0.5).then_inc(exp_done, 1)
                        st += 1
                    if kind == "pv" and s[2:] == (TT - 1, GH - 1):
                        g = s[1]
                        act.wait_ge(pv_done, t.b * GROUPS + (g + 1))
                        nc.scalar.activation(oraw[:, g % 2, :], ps_o[:, g % 2, :], ACT.Copy).then_inc(o_raw, 1)

            turns(act, run)

        @block.vector
        def _(dve):
            nc.vector.memset(qst[:, :, :, :].bitcast(F32), 0.0)
            nc.vector.memset(kst[0:MAXROW, :, :, :].bitcast(F32), 0.0)
            nc.vector.memset(kst[MAXROW:P, :, :, :].bitcast(F32), 1.0).then_inc(prep_dve, 1)
            chain = 0
            if cross:
                dve.wait_ge(w_loaded, 16 * 9)
                nc.vector.tensor_scalar(out=lower[:, :, :], in0=room[:, 2048:2560].bitcast(U8).rearrange("p (a c) -> p a c", a=TT),
                                        scalar1=BIG, scalar2=-BIG, op0=ALU.mult, op1=ALU.add)
                nc.vector.memset(ones[:, :], 1.0)
                nc.vector.tensor_scalar(out=lower_t[:, :, :], in0=room[:, 2560:3072].bitcast(U8).rearrange("p (a c) -> p a c", a=TT),
                                        scalar1=1.0, scalar2=None, op0=ALU.mult).then_inc(prep_dve, 1)
                dve.wait_ge(prep_mm, 1)
                nc.vector.tensor_scalar(out=some_key[:, :], in0=ps_p1[:, 0, :], scalar1=1.0, scalar2=None, op0=ALU.min)
                nc.vector.tensor_scalar(out=lower_t[:, :, :], in0=room[:, 2560:3072].bitcast(U8).rearrange("p (a c) -> p a c", a=TT),
                                        scalar1=BIG, scalar2=-BIG, op0=ALU.mult, op1=ALU.add).then_inc(prep_dve, 1)
                dve.wait_ge(prep_act, 1)
                for i, (hi, lo) in enumerate(((wqk[:, 0, 0], wqk[:, 1, 0]), (wqk[:, 0, 1], wqk[:, 1, 1]), (wv[:, 0], wv[:, 1]), (wo[:, 0], wo[:, 1]))):
                    last = nc.vector.tensor_tensor(out=lo, in0=room[:, i * 512:(i + 1) * 512].rearrange("p (a c) -> p a c", a=KT),
                                                   in1=hi.bitcast(F32), op=ALU.subtract)
                last.then_inc(prep_dve, 1)
            else:
                dve.wait_ge(prep_act, 1)
                for side in range(2):
                    for ct in range(KT):
                        for tile in range(2):
                            src = ps_p1[:, side, ct * C:(ct + 1) * C].rearrange("p (m j t d) -> p t m j d", m=2, j=8, t=2)[:, tile]
                            nc.vector.tensor_tensor(out=head_order(wqk[:, 1, side, ct, :], tile), in0=src,
                                                    in1=head_order(wqk[:, 0, side, ct, :], tile).bitcast(F32), op=ALU.subtract)
                nc.vector.tensor_tensor(out=wv[:, 1, :, :], in0=ps_st[:, 0, :].rearrange("p (a c) -> p a c", a=KT),
                                        in1=wv[:, 0, :, :].bitcast(F32), op=ALU.subtract)
                nc.vector.tensor_tensor(out=wo[:, 1, :, :], in0=room[:, 6144:6656].rearrange("p (a c) -> p a c", a=KT),
                                        in1=wo[:, 0, :, :].bitcast(F32), op=ALU.subtract).then_inc(prep_dve, 3)
            dve.wait_ge(consts, 2)

            def high_first(s):
                return s[0] in H_KINDS and not (s[0] == "qk" and (s[1] == 0 if cross else s[2] == 1))

            def run(t, steps):
                chain, m, p1, hd, tiles = 0, 0, 0, 0, 0
                c0 = before(t.b, lambda x: count(x, ("ln", "neg", "og")))
                mb = before(t.b, lambda x: sum(high_first(s) for s in x))
                for s in steps:
                    kind = s[0]
                    if kind == "ln":
                        dve.wait_ge(x_loaded, t.nxt * 16 + 16)
                        if t.b is not None:
                            dve.wait_ge(xn_ready, t.nxt)
                        for tt in range(TT):
                            last = nc.vector.bn_stats(stats[:, tt, :], xin[:, tt, :])
                        last.then_inc(dve_chain, 1)
                        chain += 1
                        dve.wait_ge(dve_chain, c0 + chain)
                        dve.sem_inc(held, 1)
                        for tt in range(TT):
                            last = nc.vector.bn_aggr(mv[:, tt, :], stats[:, tt, :])
                        last.then_inc(stats_ready, 1)
                    if kind == "p1":
                        g, j, qt = s[1], s[2], s[3]
                        n = keys_of(qt)
                        add = lower[:, qt, :] if cross else lower[:, S - n:S]
                        dve.wait_ge(p1_ready, t.p1 + (p1 + 1))
                        dve.sem_inc(held, 1)
                        bank = ps_p1[:, (t.p1_par + p1) % 2, 0:n]
                        nc.vector.tensor_tensor_reduce(out=bank, in0=bank, in1=add,
                                                       scale=1.0, scalar=-3.0e38, op0=ALU.add, op1=ALU.max,
                                                       accum_out=mx[:, g % 2, j * TT + qt:j * TT + qt + 1]).then_inc(max_done, 1)
                        p1 += 1
                    elif kind == "neg":
                        g = s[1] % 2
                        dve.wait_ge(max_done, t.p1 + p1)
                        nc.vector.tensor_scalar(out=neg[:, 0, :], in0=mx[:, g, :], scalar1=-1.0, scalar2=None,
                                                op0=ALU.mult).then_inc(dve_chain, 1)
                        chain += 1
                        dve.wait_ge(dve_chain, c0 + chain)
                        nc.vector.scalar_tensor_tensor(out=neg[:, 1, :], in0=mx[:, g, :], scalar=-1.0, in1=neg[:, 0, :].bitcast(F32),
                                                       op0=ALU.mult, op1=ALU.subtract).then_inc(neg_ready, 1)
                    if kind not in M_KINDS:
                        continue
                    bank = ps_m[:, (t.m_par + m) % 2, :]
                    dve.wait_ge(m_ready, t.m + (m + 1))
                    m += 1
                    pooled = kind == "qk" and (s[1] == 0 if cross else s[2] == 1)
                    if kind in H_KINDS and not pooled:
                        hd += 1
                        dve.wait_ge(h_done, mb + hd)
                    if kind in ("xt", "ot"):
                        hi, lo = (xt_h, xt_l) if kind == "xt" else (ot_h, ot_l)
                        nc.vector.tensor_tensor(out=lo[:, s[1], :], in0=bank, in1=hi[:, s[1], :].bitcast(F32),
                                                op=ALU.subtract).then_inc(m_free, 1)
                    elif kind == "qk" and pooled:
                        if not (t.b is None and tiles == 0):
                            dve.wait_ge(q_pool, t.nxt * POOL_TILES + tiles)
                        tiles += 1
                        if cross:
                            nc.vector.scalar_tensor_tensor(out=qtmp[:, :], in0=bank, scalar=bqk[:, s[1], s[2]:s[2] + 1],
                                                           in1=some_key[:, :], op0=ALU.add, op1=ALU.mult).then_inc(m_free, 1)
                        else:
                            nc.vector.tensor_tensor(out=rope_a[:, :], in0=bank, in1=cosb[:, :], op=ALU.mult)
                            nc.vector.stream_shuffle(rope_b[:, :], bank, [i ^ 8 for i in range(32)]).then_inc(m_free, 1)
                    elif kind == "qk":
                        if cross:
                            nc.vector.scalar_tensor_tensor(out=qk_l[:, s[1], s[2], :], in0=bank, scalar=bqk[:, s[1], s[2]:s[2] + 1],
                                                           in1=qk_h[:, s[1], s[2], :].bitcast(F32), op0=ALU.add,
                                                           op1=ALU.subtract).then_inc(m_free, 1)
                        else:
                            nc.vector.tensor_tensor(out=qk_l[:, s[1], s[2], :], in0=bank, in1=qk_h[:, s[1], s[2], :].bitcast(F32),
                                                    op=ALU.subtract).then_inc(m_free, 1)
                    elif kind == "v":
                        for i in range(2):
                            out = vals[:, 2 * s[1] + i, :, 0:DH]
                            src = bank[:, i * C:(i + 1) * C].rearrange("p (h d) -> p h d", h=H)
                            if cross:
                                last = nc.vector.tensor_tensor(out=out, in0=src, in1=bv[:, :].rearrange("p (h d) -> p h d", h=H), op=ALU.add)
                            else:
                                last = nc.vector.tensor_copy(out, src)
                        last.then_inc(m_free, 1)
                    elif kind == "mt":
                        if t.b is not None:
                            dve.wait_ge(shifted, t.b * (16 * GROUPS) + 16 * s[1])
                        nc.vector.tensor_copy(shift[:, :], bank[0:32, 0:P]).then_inc(m_free, 1)
                    elif kind == "og":
                        g = s[1]
                        view = bank.rearrange("p (q d) -> p q d", d=32)
                        nc.vector.reciprocal(rec[:, g % 2, :], view[:, :, DH]).then_inc(dve_chain, 1)
                        chain += 1
                        dve.wait_ge(dve_chain, c0 + chain)
                        nc.vector.tensor_tensor(
                            out=ocomp[:, :, (g % GROUPS) * GH * DH:(g % GROUPS + 1) * GH * DH].rearrange("p q (j d) -> p q j d", d=DH),
                            in0=bank.rearrange("p (q j d) -> p q j d", q=TT, d=32)[:, :, :, 0:DH],
                            in1=rec[:, g % 2, :].rearrange("p (q j) -> p q j", q=TT).unsqueeze(3).to_broadcast([P, TT, GH, DH]),
                            op=ALU.mult).then_inc(m_free, 1)
                    elif kind == "y":
                        if s[1] == 0:
                            if cross:
                                dve.wait_ge(res_bias, t.b + (s[2] + 1))
                            else:
                                dve.wait_ge(xres_loaded, t.b * 16 + 16 * (s[2] + 1))
                        res = xres[:, 2 * s[1]:2 * s[1] + 2, :]
                        nc.vector.tensor_tensor(out=res, in0=bank.rearrange("p (i c) -> p i c", i=2), in1=res,
                                                op=ALU.add).then_inc(m_free, 1)

            turns(dve, run)


def mixture(nc, x, out, table, dram, ident):
    ctx = ExitStack()
    with ctx:
        def sb(n, shape, dt):
            return ctx.enter_context(nc.sbuf_tensor(f"moe_{n}", shape, dt))

        def sem(n):
            return ctx.enter_context(nc.semaphore(f"moe_{n}"))

        FT = DFF // P
        CT = CAP // P
        HI, LO = 32, 16
        BITS = 30
        SC = E_N * NT

        xin = sb("xin", [P, 2, TT, C], F32)
        xn = sb("xn", [P, 2, TT, C], F32)
        stats = sb("stats", [P, 2, TT, 6], F32)
        mv = sb("mv", [P, 2, TT, 2], F32)
        lnw = sb("lnw", [P, 4, TT], F32)
        half_neg = sb("half_neg", [P, TT], F32)
        xnt = sb("xnt", [P, 2, KT, S], F32)
        rw = sb("rw", [P, KT, E_N], F32)
        rb = sb("rb", [P, E_N], F32)
        logits = sb("logits", [P, NT, E_N], F32)
        top = sb("top", [P, NT], F32)
        tot = sb("tot", [P, NT], F32)
        score = sb("score", [P, E_N, NT], F32)
        bit = sb("bit", [P, E_N], I32)
        thr = sb("thr", [P, E_N], I32)
        cand = sb("cand", [P, E_N], I32)
        won = sb("won", [P, E_N], I32)
        ge = sb("ge", [P, E_N, NT], BF16)
        cnt = sb("cnt", [P, E_N], BF16)
        above = sb("above", [P, E_N, NT], BF16)
        tied = sb("tied", [P, E_N, NT], BF16)
        need = sb("need", [P, E_N], F32)
        scan = sb("scan", [P, SC], F32)
        restart = sb("restart", [P, E_N, NT], F32)
        rank = sb("rank", [P, SC], F32)
        picked = sb("picked", [P, E_N, NT], BF16)
        place = sb("place", [P, E_N, NT], I32)
        place_hi = sb("place_hi", [P, E_N, NT], I32)
        place_lo = sb("place_lo", [P, E_N, NT], I32)
        ones = sb("ones", [P, P], BF16)
        before = sb("before", [P, P], BF16)
        iota = sb("iota", [P, HI], I32)
        tile_no = sb("tile_no", [P, NT], I32)
        part_no = sb("part_no", [P, 1], F32)
        part_i = sb("part_i", [P, 1], I32)
        hot_hi = sb("hot_hi", [P, 2, NT, HI], BF16)
        hot_lo = sb("hot_lo", [P, 2, NT, LO], BF16)
        hot_id = sb("hot_id", [P, 2, NT, 2, LO], BF16)
        id_part = sb("id_part", [HI, 2, LO], F32)
        id_tok = sb("id_tok", [HI, 2, LO], I32)
        ids = sb("ids", [P, 2, CT], I32)
        w1r = sb("w1r", [P, 2, KT, DFF], F32)
        w2r = sb("w2r", [P, 2, FT, C], F32)
        w1 = sb("w1", [P, 2, 2, KT, DFF], F32R)
        w2 = sb("w2", [P, 2, 2, FT, C], F32R)
        b1 = sb("b1", [P, E_N, FT], F32)
        b2 = sb("b2", [P, E_N, C], F32)
        tok = sb("tok", [P, 2, CT, ROW], F32)
        tok_h = sb("tok_h", [P, 2, KT, CAP], F32R)
        tok_l = sb("tok_l", [P, 2, KT, CAP], F32R)
        relu = sb("relu", [P, 2, CAP], F32)
        hid_h = sb("hid_h", [P, 4, CAP], F32R)
        hid_l = sb("hid_l", [P, 4, CAP], F32R)
        part = sb("part", [P, CT, C], F32)

        ps_a = ctx.enter_context(nc.psum_tensor("moe_ps_a", [P, 2, S], F32))
        ps_h = ctx.enter_context(nc.psum_tensor("moe_ps_h", [P, 2, S], F32))
        ps_y = ctx.enter_context(nc.psum_tensor("moe_ps_y", [P, CT, S], F32))

        held = sem("held")
        x_loaded = [sem(f"x_loaded_{q}") for q in range(2)]
        in_loaded = sem("in_loaded")
        consts = sem("consts")
        pool_chain = sem("pool_chain")
        dve_chain = sem("dve_chain")
        stats_ready = sem("stats_ready")
        xn_ready = sem("xn_ready")
        xt_ready = sem("xt_ready")
        xt_taken = sem("xt_taken")
        lg_ready = sem("lg_ready")
        lg_taken = sem("lg_taken")
        rows_stored = [sem(f"rows_stored_{q}") for q in range(2)]
        scores_stored = sem("scores_stored")
        scored = sem("scored")
        exp_in = sem("exp_in")
        exp_out = sem("exp_out")
        cnt_ready = sem("cnt_ready")
        cnt_sum = sem("cnt_sum")
        pre_in = sem("pre_in")
        pre_out = sem("pre_out")
        hot_ready = sem("hot_ready")
        id_sum = sem("id_sum")
        id_free = sem("id_free")
        id_ready = sem("id_ready")
        ids_moved = sem("ids_moved")
        gathered = sem("gathered")
        w_loaded = [sem(f"w_loaded_{q}") for q in range(2)]
        w_high = sem("w_high")
        w1_low = sem("w1_low")
        w2_low = sem("w2_low")
        t_ready = sem("t_ready")
        t_high = sem("t_high")
        t_free = sem("t_free")
        g_ready = sem("g_ready")
        relu_done = sem("relu_done")
        hid_high = sem("hid_high")
        hid_low = sem("hid_low")
        y_ready = sem("y_ready")
        y_free = sem("y_free")
        weighted = sem("weighted")
        scattered = sem("scattered")
        part_free = sem("part_free")

        x_v = x.rearrange("(b t p) c -> b p t c", b=B, p=P)
        table_v = table.rearrange("(b t p) c -> b p t c", b=B, p=P)
        block = ctx.enter_context(nc.Block())

        @block.sync
        def _(sp):
            sp.dma_start(rw[:, :, :], dram["router_w"].rearrange("(k p) e -> p k e", p=P)).then_inc(in_loaded, 16)
            sp.dma_start(rb[:, :], dram["router_b"].partition_broadcast(P)).then_inc(in_loaded, 16)

            def router(b, q):
                sp.wait_ge(xn_ready, b + 1)
                sp.sem_inc(held, 1)
                sp.dma_start(table_v[b][:, :, 0:C], xn[:, q, :, :]).then_inc(rows_stored[q], 16)

            for q in range(2):
                sp.dma_start(xin[:, q, :, :], x_v[q]).then_inc(x_loaded[q], 16)
            sp.dma_start(b1[:, :, :], dram["b1"]).then_inc(in_loaded, 16)
            sp.dma_start(b2[:, :, :], dram["b2"].partition_broadcast(P)).then_inc(in_loaded, 16)
            with sp.Fori(0, B // 2 - 1) as i:
                for q in range(2):
                    router(i * 2 + q, q)
                    sp.dma_start(xin[:, q, :, :], x_v[i * 2 + (q + 2)]).then_inc(x_loaded[q], 16)
            for q in range(2):
                router(B - 2 + q, q)

            def weights(e, q):
                sp.dma_start(w1r[:, q, :, :], dram["w1"][e].rearrange("(k p) f -> p k f", p=P)).then_inc(w_loaded[q], 16)
                sp.dma_start(w2r[:, q, :, :], dram["w2"][e].rearrange("(k p) f -> p k f", p=P)).then_inc(w_loaded[q], 16)

            weights(0, 0)
            weights(1, 1)
            sp.wait_ge(scored, 1)
            with nc.allow_non_contiguous_dma(reason="8 scores of a row"):
                sp.dma_start(table.rearrange("(t p) c -> p t c", p=P)[:, :, C:C + E_N], logits[:, :, :]).then_inc(scores_stored, 16)

            def listed(e, q):
                sp.wait_ge(id_ready, e + 1)
                sp.sem_inc(held, 1)
                sp.dma_start(ids[:, q, :], id_tok[:, q, :]).then_inc(ids_moved, 16)

            def expert(e, q, nxt, more):
                if nxt:
                    sp.wait_ge(part_free, e + 1)
                    sp.sem_inc(held, 1)
                    listed(e + 1, 1 - q)
                if more:
                    sp.wait_ge(w_high, e * 4 + 4)
                    sp.sem_inc(held, 1)
                    sp.wait_ge(w1_low, e + 1)
                    sp.sem_inc(held, 1)
                    sp.wait_ge(w2_low, e * 2 + 2)
                    sp.sem_inc(held, 1)
                    weights(e + 2, q)

            listed(0, 0)
            with sp.Fori(0, E_N // 2 - 1) as i:
                for q in range(2):
                    expert(i * 2 + q, q, True, True)
            expert(E_N - 2, 0, True, False)

        @block.gpsimd
        def _(pool):
            n = 0
            for op in (
                lambda: nc.gpsimd.memset(half_neg[:, :], -0.5),
                lambda: nc.gpsimd.memset(ones[:, :], 1.0),
                lambda: nc.gpsimd.memset(before[:, :], 1.0),
                lambda: nc.gpsimd.affine_select(out=before[:, :], in_=before[:, :], compare_op=ALU.is_gt, fill=0.0,
                                                base=0, pattern=[[1, P]], channel_multiplier=-1),
                lambda: nc.gpsimd.iota(iota[:, :], pattern=[[1, HI]], base=0, channel_multiplier=0),
                lambda: nc.gpsimd.iota(tile_no[:, :], pattern=[[1, NT]], base=0, channel_multiplier=0),
                lambda: nc.gpsimd.iota(part_i[:, :], pattern=[[1, 1]], base=0, channel_multiplier=1),
                lambda: nc.gpsimd.tensor_copy(part_no[:, :], part_i[:, :]),
                lambda: nc.gpsimd.memset(restart[:, :, :], 1.0),
                lambda: nc.gpsimd.memset(restart[:, :, 0:1], 0.0),
            ):
                n += 1
                op().then_inc(pool_chain, 1)
                pool.wait_ge(pool_chain, n)
            pool.sem_inc(consts, 1)

            def norm(b, q, chain, first=False):
                pool.wait_ge(stats_ready, b + 1)
                pool.sem_inc(held, 1)
                v, y, a, m = (lnw[:, i, :] for i in range(4))
                seq = (
                    lambda: nc.gpsimd.tensor_scalar(out=v, in0=mv[:, q, :, 1], scalar1=1.0, scalar2=EPS, op0=ALU.mult, op1=ALU.add),
                    lambda: nc.gpsimd.tensor_tensor(out=y, in0=v, in1=half_neg[:, :], op=ALU.pow),
                    lambda: nc.gpsimd.tensor_tensor(out=a, in0=y, in1=y, op=ALU.mult),
                    lambda: nc.gpsimd.tensor_tensor(out=a, in0=a, in1=v, op=ALU.mult),
                    lambda: nc.gpsimd.tensor_scalar(out=a, in0=a, scalar1=-0.5, scalar2=1.5, op0=ALU.mult, op1=ALU.add),
                    lambda: nc.gpsimd.tensor_tensor(out=y, in0=y, in1=a, op=ALU.mult),
                    lambda: nc.gpsimd.tensor_tensor(out=m, in0=mv[:, q, :, 0], in1=y, op=ALU.mult),
                    lambda: nc.gpsimd.tensor_scalar(out=m, in0=m, scalar1=-1.0, scalar2=0.0, op0=ALU.mult, op1=ALU.add),
                )
                for i, op in enumerate(seq):
                    op().then_inc(pool_chain, 1)
                    pool.wait_ge(pool_chain, chain + (i + 1))
                    pool.sem_inc(held, 1)
                pool.wait_ge(xt_taken, b + 1)
                pool.sem_inc(held, 1)
                if not first:
                    pool.wait_ge(rows_stored[q], b * 8 - 8 * q)
                    pool.sem_inc(held, 1)
                for t in range(TT):
                    last = nc.gpsimd.tensor_scalar(out=xn[:, q, t, :], in0=xin[:, q, t, :], scalar1=y[:, t:t + 1],
                                                   scalar2=m[:, t:t + 1], op0=ALU.mult, op1=ALU.add)
                last.then_inc(xn_ready, 1)

            pool.sem_inc(part_free, 1)
            for q in range(2):
                norm(q, q, n + 8 * q, True)
            with pool.Fori(1, B // 2) as i:
                for q in range(2):
                    norm(i * 2 + q, q, i * 16 + (n + 8 * q))

            def low_w1(e, q):
                pool.wait_ge(w_high, e * 4 + 2)
                nc.gpsimd.tensor_tensor(out=w1[:, q, 1, :, :], in0=w1r[:, q, :, :], in1=w1[:, q, 0, :, :].bitcast(F32),
                                        op=ALU.subtract).then_inc(w1_low, 1)

            def gather(e, q):
                pool.wait_ge(ids_moved, e * 16 + 16)
                pool.sem_inc(held, 1)
                for c in range(CT):
                    nc.gpsimd.indirect_dma_start(out=tok[:, q, c, :], out_offset=None, in_=table[:, :],
                                                 in_offset=bass.IndirectOffsetOnAxis(ap=ids[:, q, c:c + 1], axis=0)
                                                 ).then_inc(gathered, 16)

            def scatter(e, q):
                for c in range(CT):
                    pool.wait_ge(weighted, e * CT + (c + 1))
                    pool.sem_inc(held, 1)
                    nc.gpsimd.indirect_dma_start(out=out[:, :], out_offset=bass.IndirectOffsetOnAxis(ap=ids[:, q, c:c + 1], axis=0),
                                                 in_=part[:, c, :], in_offset=None, compute_op=ALU.add).then_inc(scattered, 16)

            low_w1(0, 0)
            for q in range(2):
                pool.wait_ge(rows_stored[q], B // 2 * 16)
            pool.wait_ge(scores_stored, 16)
            gather(0, 0)

            def expert(e, q, nxt):
                if nxt:
                    gather(e + 1, 1 - q)
                    low_w1(e + 1, 1 - q)
                scatter(e, q)
                pool.wait_ge(scattered, e * (16 * CT) + 16 * CT)
                pool.sem_inc(part_free, 1)

            with pool.Fori(0, E_N // 2 - 1) as i:
                for q in range(2):
                    expert(i * 2 + q, q, True)
            expert(E_N - 2, 0, True)
            expert(E_N - 1, 1, False)

        @block.tensor
        def _(pe):
            pe.sem_inc(xt_taken, 2)
            pe.wait_ge(in_loaded, 64)

            def router(b, q):
                pe.wait_ge(xn_ready, b + 1)
                pe.wait_ge(xt_taken, b + 2)
                pe.wait_ge(lg_taken, b + 1)
                for k in range(KT):
                    for t in range(TT):
                        last = nc.tensor.transpose(ps_a[:, k, t * P:(t + 1) * P], xn[:, q, t, k * P:(k + 1) * P], ident[:, :])
                last.then_inc(xt_ready, 1)
                pe.wait_ge(xt_taken, b + 3)
                for t in range(TT):
                    for k in range(KT):
                        last = nc.tensor.matmul(ps_h[:, q, t * E_N:(t + 1) * E_N], xnt[:, q, k, t * P:(t + 1) * P], rw[:, k, :],
                                                start=(k == 0), stop=(k == KT - 1))
                last.then_inc(lg_ready, 1)

            with pe.Fori(0, B // 2) as i:
                for q in range(2):
                    router(i * 2 + q, q)

            pe.wait_ge(consts, 1)

            def totals(k):
                pe.wait_ge(cnt_ready, k)
                nc.tensor.matmul(ps_h[:, 0, 0:E_N], ones[:, :], cnt[:, :], start=True, stop=True).then_inc(cnt_sum, 1)

            with pe.Fori(0, BITS) as i:
                totals(i + 1)
            totals(BITS + 1)
            for k, flags in ((1, tied), (2, picked)):
                pe.wait_ge(pre_in, k)
                nc.tensor.matmul(ps_a[:, 0, 0:SC], before[:, :], flags[:, :, :].rearrange("p e t -> p (e t)"), start=True, stop=True)
                nc.tensor.matmul(ps_a[:, 1, 0:SC], ones[:, :], flags[:, :, :].rearrange("p e t -> p (e t)"),
                                 start=True, stop=True).then_inc(pre_out, 1)

            def list_ids(e, q):
                pe.wait_ge(hot_ready, e + 1)
                pe.wait_ge(id_free, e + 1)
                for t in range(NT):
                    last = nc.tensor.matmul(ps_a[0:HI, 0, 0:2 * LO], hot_hi[:, q, t, :], hot_id[:, q, t, :, :].rearrange("p a b -> p (a b)"),
                                            start=(t == 0), stop=(t == NT - 1))
                last.then_inc(id_sum, 1)

            def turn_tokens(e, q):
                pe.wait_ge(gathered, e * (16 * CT) + 16 * CT)
                for k in range(KT):
                    pe.wait_ge(t_free, e * KT + (k + 1))
                    if k == 0:
                        pe.wait_ge(id_free, e + 2)
                    for c in range(CT):
                        last = nc.tensor.transpose(ps_a[:, k, c * P:(c + 1) * P], tok[:, q, c, k * P:(k + 1) * P], ident[:, :])
                    last.then_inc(t_ready, 1)

            def hidden(e, q, ft):
                pe.wait_ge(relu_done, e * FT + (ft + 1))
                n = 0
                for k in range(KT):
                    for wp, xp in ((0, tok_h), (0, tok_l), (1, tok_h)):
                        last = nc.tensor.matmul(ps_h[:, ft % 2, :], w1[:, q, wp, k, ft * P:(ft + 1) * P], xp[:, q, k, :],
                                                start=(n == 0), stop=(n == 3 * KT - 1))
                        n += 1
                last.then_inc(g_ready, 1)

            def result(e, q, ft):
                pe.wait_ge(hid_low, e * FT + (ft + 3))
                if ft == 0:
                    pe.wait_ge(y_free, e + 1)
                for c in range(CT):
                    at = slice(c * P, (c + 1) * P)
                    for n, (xp, wp) in enumerate(((hid_h, 0), (hid_h, 1), (hid_l, 0))):
                        last = nc.tensor.matmul(ps_y[:, c, 0:C], xp[:, ft % 4, at], w2[:, q, wp, ft, :],
                                                start=(ft == 0 and n == 0), stop=(ft == FT - 1 and n == 2))
                last.then_inc(y_ready, 1)

            def expert(e, q, nxt):
                pe.wait_ge(w1_low, e + 1)
                pe.wait_ge(w2_low, e * 2 + 2)
                pe.wait_ge(t_free, e * KT + (2 + KT))
                for ft in range(FT):
                    hidden(e, q, ft)
                    if ft:
                        result(e, q, ft - 1)
                    if nxt and ft == 2:
                        list_ids(e + 1, 1 - q)
                    if nxt and ft == FT - 2:
                        turn_tokens(e + 1, 1 - q)
                result(e, q, FT - 1)

            list_ids(0, 0)
            turn_tokens(0, 0)
            with pe.Fori(0, E_N // 2 - 1) as i:
                for q in range(2):
                    expert(i * 2 + q, q, True)
            expert(E_N - 2, 0, True)
            expert(E_N - 1, 1, False)

        @block.scalar
        def _(act):
            act.sem_inc(relu_done, 2)
            with act.Fori(0, B // 2) as i:
                for q in range(2):
                    act.wait_ge(xt_ready, i * 2 + (q + 1))
                    nc.scalar.activation(xnt[:, q, :, :], ps_a[:, :, :], ACT.Copy).then_inc(xt_taken, 1)

            def high_w(e, q, part):
                if part == 0:
                    act.wait_ge(w_loaded[q], e * 16 + (32 - 16 * q))
                if part < 2:
                    nc.scalar.activation(w1[:, q, 0, part, :], w1r[:, q, part, :], ACT.Copy).then_inc(w_high, 1)
                else:
                    at = slice((part - 2) * FT // 2, (part - 1) * FT // 2)
                    nc.scalar.activation(w2[:, q, 0, at, :], w2r[:, q, at, :], ACT.Copy).then_inc(w_high, 1)

            act.wait_ge(exp_in, 1)
            nc.scalar.activation(logits[:, :, :], logits[:, :, :], ACT.Exp).then_inc(exp_out, 1)
            for part in range(4):
                high_w(0, 0, part)

            def high_tokens(e, q):
                for k in range(KT):
                    act.wait_ge(t_ready, e * KT + (k + 1))
                    nc.scalar.activation(tok_h[:, q, k, :], ps_a[:, k, :], ACT.Copy).then_inc(t_high, 1)

            def expert(e, q, nxt):
                for ft in range(FT):
                    act.wait_ge(g_ready, e * FT + (ft + 1))
                    act.wait_ge(hid_low, e * FT + (ft + 1))
                    nc.scalar.activation(relu[:, ft % 2, :], ps_h[:, ft % 2, :], ACT.Relu,
                                         bias=b1[:, e, ft:ft + 1]).then_inc(relu_done, 1)
                    if nxt and ft == 1:
                        act.wait_ge(y_ready, e * FT + 1)
                    if nxt and 1 <= ft <= 4:
                        high_w(e + 1, 1 - q, ft - 1)
                    if nxt and ft == FT - 2:
                        high_tokens(e + 1, 1 - q)

            high_tokens(0, 0)
            with act.Fori(0, E_N // 2 - 1) as i:
                for q in range(2):
                    expert(i * 2 + q, q, True)
            expert(E_N - 2, 0, True)
            expert(E_N - 1, 1, False)

        @block.vector
        def _(dve):
            dve.sem_inc(lg_taken, 1)
            dve.sem_inc(lg_taken, 1)
            dve.sem_inc(t_free, 2)
            dve.sem_inc(id_free, 1)
            dve.sem_inc(y_free, 1)
            dve.sem_inc(hid_low, 2)
            n = [0]

            def link(ins):
                n[0] += 1
                ins.then_inc(dve_chain, 1)
                dve.wait_ge(dve_chain, n[0])

            dve.wait_ge(in_loaded, 64)

            def router(b, q, chain):
                dve.wait_ge(x_loaded[q], b * 8 + (16 - 8 * q))
                for t in range(TT):
                    last = nc.vector.bn_stats(stats[:, q, t, :], xin[:, q, t, :])
                last.then_inc(dve_chain, 1)
                dve.wait_ge(dve_chain, chain + 1)
                dve.sem_inc(held, 1)
                for t in range(TT):
                    last = nc.vector.bn_aggr(mv[:, q, t, :], stats[:, q, t, :])
                last.then_inc(stats_ready, 1)

            def take_logits(b, q):
                dve.wait_ge(lg_ready, b + 1)
                nc.vector.tensor_tensor(out=logits[:, bass.ds(b * TT, TT), :],
                                        in0=ps_h[:, q, 0:TT * E_N].rearrange("p (t e) -> p t e", e=E_N),
                                        in1=rb[:, :].unsqueeze(1).to_broadcast([P, TT, E_N]), op=ALU.add).then_inc(lg_taken, 1)

            with dve.Fori(0, B // 2) as i:
                for q in range(2):
                    router(i * 2 + q, q, i * 2 + q)
                for q in range(2):
                    take_logits(i * 2 + q, q)
            n[0] = B

            dve.wait_ge(lg_taken, B + 2)
            link(nc.vector.tensor_reduce(top[:, :], logits[:, :, :], AX.X, ALU.max))
            nc.vector.tensor_tensor(out=logits[:, :, :], in0=logits[:, :, :], in1=top[:, :].unsqueeze(2).to_broadcast([P, NT, E_N]),
                                    op=ALU.subtract).then_inc(exp_in, 1)
            dve.wait_ge(exp_out, 1)
            link(nc.vector.tensor_reduce(tot[:, :], logits[:, :, :], AX.X, ALU.add))
            link(nc.vector.reciprocal(tot[:, :], tot[:, :]))
            nc.vector.tensor_tensor(out=logits[:, :, :], in0=logits[:, :, :], in1=tot[:, :].unsqueeze(2).to_broadcast([P, NT, E_N]),
                                    op=ALU.mult).then_inc(scored, 1)
            dve.wait_ge(scored, 1)
            dve.wait_ge(consts, 1)
            nc.vector.memset(bit[:, :], 1 << (BITS - 1))
            nc.vector.memset(thr[:, :], 0)
            link(nc.vector.tensor_copy(score[:, :, :], logits[:, :, :].rearrange("p t e -> p e t")))

            STEPS = 5
            base = n[0]

            def step(chain):
                k = [0]

                def after(ins):
                    k[0] += 1
                    ins.then_inc(dve_chain, 1)
                    dve.wait_ge(dve_chain, chain + k[0])

                after(nc.vector.tensor_tensor(out=cand[:, :], in0=thr[:, :], in1=bit[:, :], op=ALU.bitwise_or))
                after(nc.vector.tensor_tensor(out=ge[:, :, :], in0=score[:, :, :],
                                              in1=cand[:, :].bitcast(F32).unsqueeze(2).to_broadcast([P, E_N, NT]), op=ALU.is_ge))
                return k, after

            with dve.Fori(0, BITS) as i:
                k, after = step(i * STEPS + base)
                with nc.allow_low_precision("counts up to 32 are exact"):
                    nc.vector.tensor_reduce(cnt[:, :], ge[:, :, :], AX.X, ALU.add).then_inc(cnt_ready, 1)
                dve.wait_ge(cnt_sum, i + 1)
                after(nc.vector.scalar_tensor_tensor(out=won[:, :], in0=ps_h[:, 0, 0:E_N], scalar=float(CAP), in1=bit[:, :],
                                                     op0=ALU.is_ge, op1=ALU.mult))
                nc.vector.tensor_scalar(out=bit[:, :], in0=bit[:, :], scalar1=1, scalar2=None,
                                        op0=ALU.logical_shift_right).then_inc(dve_chain, 1)
                nc.vector.tensor_tensor(out=thr[:, :], in0=thr[:, :], in1=won[:, :], op=ALU.bitwise_or).then_inc(dve_chain, 1)
                dve.wait_ge(dve_chain, i * STEPS + (base + STEPS))
            n[0] = base + BITS * STEPS

            def at_thr():
                return thr[:, :].bitcast(F32).unsqueeze(2).to_broadcast([P, E_N, NT])

            link(nc.vector.tensor_tensor(out=above[:, :, :], in0=score[:, :, :], in1=at_thr(), op=ALU.is_gt))
            nc.vector.tensor_tensor(out=tied[:, :, :], in0=score[:, :, :], in1=at_thr(), op=ALU.is_equal).then_inc(pre_in, 1)
            with nc.allow_low_precision("counts up to 32 are exact"):
                nc.vector.tensor_reduce(cnt[:, :], above[:, :, :], AX.X, ALU.add).then_inc(cnt_ready, 1)
            dve.wait_ge(cnt_sum, BITS + 1)
            link(nc.vector.tensor_scalar(out=need[:, :], in0=ps_h[:, 0, 0:E_N], scalar1=-1.0, scalar2=float(CAP), op0=ALU.mult, op1=ALU.add))

            def ranks(k):
                dve.wait_ge(pre_out, k)
                link(nc.vector.tensor_tensor_scan(out=scan[:, :], data0=restart[:, :, :].rearrange("p e t -> p (e t)"),
                                                  data1=ps_a[:, 1, 0:SC], initial=0.0, op0=ALU.mult, op1=ALU.add))
                link(nc.vector.tensor_tensor(out=scan[:, :], in0=scan[:, :], in1=ps_a[:, 1, 0:SC], op=ALU.subtract))
                link(nc.vector.tensor_tensor(out=rank[:, :], in0=scan[:, :], in1=ps_a[:, 0, 0:SC], op=ALU.add))

            rank_v = rank[:, :].rearrange("p (e t) -> p e t", e=E_N)
            ranks(1)
            link(nc.vector.tensor_tensor(out=rank_v, in0=rank_v, in1=need[:, :].unsqueeze(2).to_broadcast([P, E_N, NT]), op=ALU.is_lt))
            link(nc.vector.tensor_tensor(out=rank_v, in0=rank_v, in1=tied[:, :, :], op=ALU.mult))
            nc.vector.tensor_tensor(out=picked[:, :, :], in0=rank_v, in1=above[:, :, :], op=ALU.add).then_inc(pre_in, 1)
            dve.wait_ge(pre_in, 2)
            ranks(2)
            link(nc.vector.scalar_tensor_tensor(out=rank_v, in0=rank_v, scalar=1.0, in1=picked[:, :, :], op0=ALU.add, op1=ALU.mult))
            link(nc.vector.tensor_scalar(out=place[:, :, :], in0=rank_v, scalar1=-1.0, scalar2=None, op0=ALU.add))
            link(nc.vector.tensor_scalar(out=place_hi[:, :, :], in0=place[:, :, :], scalar1=4, scalar2=None, op0=ALU.arith_shift_right))
            link(nc.vector.tensor_scalar(out=place_lo[:, :, :], in0=place[:, :, :], scalar1=LO - 1, scalar2=None, op0=ALU.bitwise_and))
            HOTS = 1
            IDS = 1

            def one_hots(e, q, chain):
                hi, lo = (v[:, e, :].unsqueeze(2) for v in (place_hi, place_lo))
                nc.vector.tensor_tensor(out=hot_hi[:, q, :, :], in0=hi.to_broadcast([P, NT, HI]),
                                        in1=iota[:, :].unsqueeze(1).to_broadcast([P, NT, HI]), op=ALU.is_equal)
                nc.vector.tensor_tensor(out=hot_lo[:, q, :, :], in0=lo.to_broadcast([P, NT, LO]),
                                        in1=iota[:, 0:LO].unsqueeze(1).to_broadcast([P, NT, LO]), op=ALU.is_equal).then_inc(dve_chain, 1)
                dve.wait_ge(dve_chain, chain + 1)
                nc.vector.tensor_tensor(out=hot_id[:, q, :, 0, :], in0=hot_lo[:, q, :, :],
                                        in1=tile_no[:, :].unsqueeze(2).to_broadcast([P, NT, LO]), op=ALU.mult)
                nc.vector.tensor_scalar(out=hot_id[:, q, :, 1, :], in0=hot_lo[:, q, :, :], scalar1=part_no[:, 0:1], scalar2=None,
                                        op0=ALU.mult).then_inc(hot_ready, 1)

            def take_ids(e, q, chain):
                dve.wait_ge(id_sum, e + 1)
                nc.vector.tensor_copy(id_part[:, q, :], ps_a[0:HI, 0, LO:2 * LO]).then_inc(dve_chain, 1)
                dve.wait_ge(dve_chain, chain + 1)
                dve.sem_inc(held, 1)
                nc.vector.scalar_tensor_tensor(out=id_tok[:, q, :], in0=ps_a[0:HI, 0, 0:LO], scalar=float(P), in1=id_part[:, q, :],
                                               op0=ALU.mult, op1=ALU.add).then_inc(id_ready, 1)
                dve.wait_ge(id_ready, e + 1)
                dve.sem_inc(id_free, 1)

            def low_w2(e, q, part):
                at = slice(part * FT // 2, (part + 1) * FT // 2)
                dve.wait_ge(w_high, e * 4 + (part + 3))
                nc.vector.tensor_tensor(out=w2[:, q, 1, at, :], in0=w2r[:, q, at, :], in1=w2[:, q, 0, at, :].bitcast(F32),
                                        op=ALU.subtract).then_inc(w2_low, 1)

            def low_tokens(e, q):
                for k in range(KT):
                    dve.wait_ge(t_high, e * KT + (k + 1))
                    nc.vector.tensor_tensor(out=tok_l[:, q, k, :], in0=ps_a[:, k, :], in1=tok_h[:, q, k, :].bitcast(F32),
                                            op=ALU.subtract).then_inc(t_free, 1)

            PER = HOTS + IDS
            e_base = n[0]
            one_hots(0, 0, e_base)
            low_w2(0, 0, 0)
            low_w2(0, 0, 1)
            take_ids(0, 0, e_base + 1)
            low_tokens(0, 0)
            e_base += PER

            def expert(e, q, nxt, chain):
                for ft in range(FT):
                    dve.wait_ge(relu_done, e * FT + (ft + 3))
                    nc.vector.tensor_copy(hid_h[:, ft % 4, :], relu[:, ft % 2, :]).then_inc(hid_high, 1)
                    dve.wait_ge(hid_high, e * FT + (ft + 1))
                    nc.vector.tensor_tensor(out=hid_l[:, ft % 4, :], in0=relu[:, ft % 2, :], in1=hid_h[:, ft % 4, :].bitcast(F32),
                                            op=ALU.subtract).then_inc(hid_low, 1)
                    if nxt and ft == 0:
                        one_hots(e + 1, 1 - q, chain)
                    if nxt and ft == 2:
                        take_ids(e + 1, 1 - q, chain + 1)
                    if nxt and 4 <= ft <= 5:
                        low_w2(e + 1, 1 - q, ft - 4)
                    if nxt and ft == FT - 2:
                        low_tokens(e + 1, 1 - q)
                dve.wait_ge(y_ready, e * FT + FT)
                dve.wait_ge(part_free, e + 1)
                for c in range(CT):
                    last = nc.vector.tensor_tensor(out=part[:, c, :], in0=ps_y[:, c, 0:C], in1=b2[:, e, :], op=ALU.add)
                last.then_inc(y_free, 1)
                dve.wait_ge(y_free, e + 2)
                dve.sem_inc(held, 1)
                for c in range(CT):
                    nc.vector.tensor_scalar(out=part[:, c, :], in0=part[:, c, :], scalar1=tok[:, q, c, bass.ds(C + e, 1)],
                                            scalar2=None, op0=ALU.mult).then_inc(weighted, 1)

            with dve.Fori(0, E_N // 2 - 1) as i:
                for q in range(2):
                    expert(i * 2 + q, q, True, i * (2 * PER) + (e_base + q * PER))
            expert(E_N - 2, 0, True, (E_N - 2) * PER + e_base)
            expert(E_N - 1, 1, False, 0)


def layout(inputs):
    import numpy as np

    def arr(k):
        return np.asarray(inputs[k])

    def stack_order(w):
        v = w.reshape(w.shape[:-1] + (2, 8, 2, 8))
        n = v.ndim
        return v.transpose(tuple(range(n - 4)) + (n - 2, n - 4, n - 1, n - 3)).reshape(w.shape)

    out = {
        "x": arr("x").reshape(NTOK, C),
        "down_t": np.stack([arr(f"L0_attn_W{k}_down").T for k in "qkv"]),
        "wc": arr("L0_attn_Wc"),
        "q_c": arr("L0_attn_Wq_up_c"), "q_e": arr("L0_attn_Wq_up_e"),
        "k_c": arr("L0_attn_Wk_up_c"), "k_e": arr("L0_attn_Wk_up_e"),
        "v_up": arr("L0_attn_Wv_up"),
        "ctx_t": arr("ctx_1024").transpose(0, 2, 1),
        "mask": arr("mask_1x1xSxS2_bk0")[0, 0],
        "mask_t": arr("mask_1x1xSxS2_bk0")[0, 0].T.copy(),
        "w_q": stack_order(arr("L0_xattn_w_q").T), "w_k": stack_order(arr("L0_xattn_w_k").T),
        "w_v": arr("L0_xattn_w_v").T, "w_o": arr("L0_xattn_w_o").T,
        "b_qk": np.stack([stack_order(arr(f"L0_xattn_b_{k}")).reshape(2, P).T for k in "qk"], axis=1),
        "b_v": arr("L0_xattn_b_v"), "b_o": arr("L0_xattn_b_o"),
        "router_w": arr("L0_ffn_router_w"), "router_b": arr("L0_ffn_router_b"),
        "w1": arr("L0_ffn_w1"), "b1": arr("L0_ffn_b1").reshape(E_N, DFF // P, P).transpose(2, 0, 1), "w2": arr("L0_ffn_w2"), "b2": arr("L0_ffn_b2"),
    }
    dim = DH // 2
    inv = (1.0 / 10000.0 ** (np.arange(0, dim, 2, dtype=np.float32) / np.float32(dim))).astype(np.float32)
    ang = np.arange(S, dtype=np.float32)[None, :] * np.concatenate((inv, inv))[:, None]
    sign = np.where(np.arange(dim) % 2 == 0, -1.0, 1.0).astype(np.float32)[:, None]
    rows = (np.arange(P) // 8) % 8
    out["cos"] = np.cos(ang).astype(np.float32)[rows]
    out["sin"] = (np.sin(ang).astype(np.float32) * sign)[rows]
    return {k: np.ascontiguousarray(v) for k, v in out.items()}


def decoder_layer(nc, dram, out, what="all"):
    with ExitStack() as ctx:
        ident = ctx.enter_context(nc.sbuf_tensor("ident", [P, P], F32))
        identb = ctx.enter_context(nc.sbuf_tensor("identb", [P, P], BF16))
        made = ctx.enter_context(nc.semaphore("ident_made"))
        with nc.Block() as block:
            @block.gpsimd
            def _(pool):
                nc.gpsimd.memset(ident[:, :], 0.0).then_inc(made, 1)
                nc.gpsimd.memset(identb[:, :], 0.0).then_inc(made, 1)
                pool.wait_ge(made, 2)
                for t in (ident, identb):
                    nc.gpsimd.affine_select(out=t[:, :], in_=t[:, :], compare_op=ALU.not_equal, fill=1.0, base=0,
                                            pattern=[[-1, P]], channel_multiplier=1).then_inc(made, 1)
                pool.wait_ge(made, 4)
        if what == "self":
            attention_layer(nc, False, dram["x"], out, dram, ident, identb)
            return
        x1 = nc.dram_tensor("x_after_self", [NTOK, C], F32).ap()
        attention_layer(nc, False, dram["x"], x1, dram, ident, identb)
        attention_layer(nc, True, x1, out, dram, ident, identb)
        if what == "cross":
            return
        table = nc.dram_tensor("rows_with_scores", [NTOK, ROW], F32).ap()
        mixture(nc, out, out, table, dram, ident)


def kernel(**inputs):
    import numpy as np
    import concourse.bacc as bacc
    from concourse.bass_utils import run_bass_kernel_spmd

    nc = bacc.Bacc("TRN2", target_bir_lowering=False, num_devices=1)
    arrays, dram = {}, {}
    for name, a in layout(inputs).items():
        arrays[f"in_{name}_dram"] = a
        dram[name] = nc.dram_tensor(f"in_{name}_dram", a.shape, mybir.dt.from_np(a.dtype), kind="ExternalInput").ap()
    out = nc.dram_tensor("out_dram", [NTOK, C], F32, kind="ExternalOutput").ap()
    decoder_layer(nc, dram, out)
    got = run_bass_kernel_spmd(nc, [arrays], core_ids=[0])
    return np.asarray(got.results[0]["out_dram"]).reshape(B, S, C)
```

```python
import concourse.bass as bass
from concourse import mybir
from contextlib import ExitStack

F32 = mybir.dt.float32
F32R = mybir.dt.float32r
BF16 = mybir.dt.bfloat16
I32 = mybir.dt.int32
U8 = mybir.dt.uint8
ALU = mybir.AluOpType
ACT = mybir.ActivationFunctionType
AX = mybir.AxisListType

P = 128
B, S, C = 8, 512, 256
H, DH = 16, 16
LAT = 64
TT = S // P
KT = C // P
GROUPS, GH = 4, 4
TERMS = 3 * DH
MAXROW = 96
STACK = MAXROW + 2
BIG = float(2 ** 30)
EPS = 1e-5
E_N, DFF, CAP = 8, 1024, 512
NT = B * TT
NTOK = B * S
ROW = C + E_N


def plan(part, router):
    nxt, prev = part != "last", part != "start"

    def p1(i):
        g, n = 1 + i // 16, i % 16
        return [("p1", g, n // TT, n % TT)] + ([("neg", g)] if n == 15 else [])

    proj = [("xt", 0), ("xt", 1), ("qk", 0, 1), ("qk", 0, 0), ("qk", 1, 1), ("qk", 1, 0)]
    if part == "first":
        out = [("ln",)] + proj
        for i in range(48, 64 + AHEAD):
            out += p1(i)
            if i == 65:
                out.append(("mt", 4))
        return out
    extra = {}

    def put(name, steps):
        for u, step in zip(SLOTS[router][name], steps):
            extra.setdefault(u, []).append(step)

    put("v", [("v", 0), ("v", 1)])
    put("og", [("og", 0), ("og", 1)])
    for g in range(GROUPS if nxt else GROUPS - 1):
        extra.setdefault(16 * (g + 1) - AHEAD + 1, []).append(("mt", g + 1))
    if router:
        put("bias", [("bias",)])
    if nxt:
        put("ln", [("ln",)])
        put("xt", proj[0:2])
        put("qk", proj[2:6])
    if prev:
        put("og_before", [("og", -2), ("og", -1)])
        put("ot", [("ot", 0, -1), ("ot", 1, -1)])
        put("y", [("y", 0, -1), ("y", 1, -1)])
        if router:
            put("ln3", [("ln3", -1)])
            put("xt3", [("xt3", 0, -1), ("xt3", 1, -1)])
            put("lg", [("lg", 0, -1), ("lg", 1, -1)])
    out = []
    for u in range(16 * GROUPS):
        g, kt, j = u // 16, u // 4 % TT, u % GH
        if g or prev:
            out.append(("pv", g - 1, kt, j))
        out.append(("st", g, kt, j))
        if nxt or u + AHEAD < 48:
            out += p1(u + AHEAD)
        out += extra.get(u, [])
    if part == "last":
        for n in range(16):
            out.append(("pv", 3, n // 4, n % 4))
            if n == 2:
                out.append(("og", 2))
        out += [("og", 3), ("ot", 0, 0), ("ot", 1, 0), ("y", 0, 0), ("y", 1, 0)]
        if router:
            out += [("ln3", 0), ("xt3", 0, 0), ("xt3", 1, 0), ("lg", 0, 0), ("lg", 1, 0)]
    return out


AHEAD = 7
SLOTS = (
    {"v": (8, 15), "ln": (5,), "xt": (16, 17), "qk": (20, 22, 26, 26), "og": (32, 49), "og_before": (2, 18),
     "ot": (29, 30), "y": (32, 33)},
    {"v": (9, 15), "ln": (5,), "xt": (16, 17), "qk": (20, 22, 26, 26), "og": (32, 49), "og_before": (1, 18),
     "ot": (27, 28), "y": (30, 32), "bias": (56,), "ln3": (33,), "xt3": (41, 43), "lg": (44, 49)},
)
M_KINDS = ("xt", "qk", "v", "mt", "og", "ot", "y", "xt3", "lg")
H_KINDS = ("xt", "qk", "ot")


def count(steps, kinds):
    return sum(s[0] in kinds for s in steps)


def m_index(steps, what):
    return count(steps[:steps.index(what)], M_KINDS)


class Schedule:

    def __init__(self, router):
        self.first, self.start, self.main, self.last = (plan(p, router) for p in ("first", "start", "main", "last"))
        assert count(self.main, M_KINDS) % 2 == 0 and count(self.main, ("p1",)) % 2 == 0

    def before(self, b, steps_of):
        if b is None:
            return 0
        if isinstance(b, int) and b == 0:
            return steps_of(self.first)
        return b * steps_of(self.main) + (steps_of(self.first) + steps_of(self.start) - steps_of(self.main))

    def turns(self, engine, run):
        run(Turn(self, 0, self.start), self.start)
        with engine.Fori(1, B - 1) as b:
            run(Turn(self, b, self.main), self.main)
        run(Turn(self, B - 1, self.last), self.last)


class Turn:

    def __init__(self, schedule, b, steps):
        self.b = b
        self.m = schedule.before(b, lambda s: count(s, M_KINDS))
        self.p1 = schedule.before(b, lambda s: count(s, ("p1",)))
        self.st = 0 if b is None else b * (16 * GROUPS)
        self.nxt = 0 if b is None else b + 1
        start = ([] if steps is schedule.first else schedule.first if steps is schedule.start
                 else schedule.first + schedule.start)
        self.m_par = count(start, M_KINDS) % 2
        self.p1_par = count(start, ("p1",)) % 2
        self.has_next = steps is not schedule.last
        self.has_prev = steps is schedule.main or steps is schedule.last
        self.loads = steps is schedule.start or steps is schedule.main


def attention_layer(nc, cross, x_in, x_out, dram, ident, identb, shared, table=None, logits=None):
    router = table is not None
    schedule = Schedule(router)
    name = "cross" if cross else "self"
    ctx = ExitStack()
    with ctx:
        def sb(n, shape, dt):
            return ctx.enter_context(nc.sbuf_tensor(f"{name}_{n}", shape, dt))

        def sem(n):
            return ctx.enter_context(nc.semaphore(f"{name}_{n}"))

        xin = sb("xin", [P, TT, C], F32)
        xres = sb("xres", [P, TT, C], F32)
        xn = sb("xn", [P, TT, C], F32)
        stats = sb("stats", [P, TT, 6], F32)
        mv = sb("mv", [P, TT, 2], F32)
        lnw = sb("lnw", [P, 5, TT], F32)
        half_neg = sb("half_neg", [P, TT], F32)
        xt_h = sb("xt_h", [P, KT, S], F32R)
        xt_l = sb("xt_l", [P, KT, S], F32R)
        qk_h = sb("qk_h", [P, 2, 2, S], F32R)
        qk_l = sb("qk_l", [P, 2, 2, S], F32R)
        qst, kst, vals = shared
        probs = sb("probs", [P, TT, GH, S], F32)
        wqk = sb("wqk", [P, 2, 2, KT, C], F32R)
        wv = sb("wv", [P, 2, KT, C], F32R)
        wo = sb("wo", [P, 2, KT, C], F32R)
        mx = sb("mx", [P, 2, 16], F32)
        neg = sb("neg", [P, 2, 16], F32R)
        shift = sb("shift", [32, P], F32R)
        ones = sb("ones", [P, P], BF16)
        oraw = sb("oraw", [P, 2, S], F32)
        ocomp = sb("ocomp", [P, TT, C], F32)
        rec = sb("rec", [P, 2, 16], F32)
        ot_h = sb("ot_h", [P, KT, S], F32R)
        ot_l = sb("ot_l", [P, KT, S], F32R)
        if cross:
            craw = sb("craw", [P, KT, S], F32)
            ct_h = sb("ct_h", [P, KT, S], F32R)
            ct_l = sb("ct_l", [P, KT, S], F32R)
            lower = sb("lower", [P, TT, S], BF16)
            lower_t = sb("lower_t", [P, TT, S], BF16)
            some_key = sb("some_key", [P, S], F32)
            bqk = sb("bqk", [P, 2, 2], F32)
            bv = sb("bv", [P, C], F32)
            bo = sb("bo", [P, C], F32)
            qtmp = sb("qtmp", [P, S], F32)
            vary = sb("vary", [1, 1], I32)
            if router:
                xnt = sb("xnt", [P, KT, S], F32)
                rw = sb("rw", [P, KT, E_N], F32)
                rb = sb("rb", [P, E_N], F32)
        else:
            cosb = sb("cosb", [P, S], F32)
            sinb = sb("sinb", [P, S], F32)
            rope_a = sb("rope_a", [P, S], F32)
            rope_b = sb("rope_b", [P, S], F32)
            lower = sb("lower", [P, S], F32)
            lower_t = sb("lower_t", [P, P], BF16)
            up = sb("up", [P, 3, 32], F32)
        room = probs[:, :, :, :].rearrange("p a b c -> p (a b c)")

        if cross:
            small = room[:, 3072:3088]
            keepers, keep_all = small[:, 0:4], small[:, 4:8]
            vary_sum, alike = small[:, 8:9], small[:, 9:10]
            differs = small[:, 10:12].bitcast(BF16)
            key_cols = room[:, 3088:3088 + TT * P // 2].bitcast(BF16).rearrange("p (a c) -> p a c", a=TT)
            key_mask = room[0:1, 3344:3344 + S]

        ps_p1 = ctx.enter_context(nc.psum_tensor(f"{name}_ps_p1", [P, 2, S], F32))
        ps_st = ctx.enter_context(nc.psum_tensor(f"{name}_ps_st", [P, 2, S], F32))
        ps_o = ctx.enter_context(nc.psum_tensor(f"{name}_ps_o", [P, 2, S], F32))
        ps_m = ctx.enter_context(nc.psum_tensor(f"{name}_ps_m", [P, 2, S], F32))

        held = sem("held")
        w_loaded = sem("w_loaded")
        consts = sem("consts")
        prep_mm = sem("prep_mm")
        prep_act = sem("prep_act")
        prep_dve = sem("prep_dve")
        ones_ready = sem("ones_ready")
        mask_chain = sem("mask_chain")
        key_row = sem("key_row")
        x_loaded = sem("x_loaded")
        xres_loaded = sem("xres_loaded")
        c_loaded = sem("c_loaded")
        stats_ready = sem("stats_ready")
        pool_chain = sem("pool_chain")
        dve_chain = sem("dve_chain")
        xn_ready = sem("xn_ready")
        ct_split = sem("ct_split")
        m_ready = sem("m_ready")
        m_free = sem("m_free")
        h_done = sem("h_done")
        q_pool = sem("q_pool")
        p1_ready = sem("p1_ready")
        max_done = sem("max_done")
        neg_ready = sem("neg_ready")
        shifted = sem("shifted")
        st_ready = sem("st_ready")
        exp_done = sem("exp_done")
        pv_done = sem("pv_done")
        o_raw = sem("o_raw")
        stacked = [sem("stacked0"), sem("stacked1")]
        res_bias = sem("res_bias")
        stats3_ready = sem("stats3_ready")
        xn3_ready = sem("xn3_ready")
        rows_stored = sem("rows_stored")
        stored = sem("stored")
        STACK_DMAS = 12
        POOL_TILES = 2

        x_in_v = x_in.rearrange("(b t p) c -> b p t c", b=B, p=P)
        x_out_v = x_out.rearrange("(b t p) c -> b p t c", b=B, p=P)
        if router:
            table_v = table.rearrange("(b t p) c -> b p t c", b=B, p=P)

        def width(kt):
            return 0 if cross else kt * P

        def keys_of(qt):
            return S if cross else (qt + 1) * P

        block = ctx.enter_context(nc.Block())

        @block.sync
        def _(sp):
            n_w = 0
            if cross:
                for i, k in enumerate(("w_q", "w_k", "w_v", "w_o")):
                    sp.dma_start(room[:, i * KT * C:(i + 1) * KT * C].rearrange("p (a c) -> p a c", a=KT),
                                 dram[k].rearrange("(a p) c -> p a c", p=P)).then_inc(w_loaded, 16)
                sp.dma_start(room[:, 2048:2560].bitcast(U8).rearrange("p (a c) -> p a c", a=TT),
                             dram["mask"].rearrange("(a p) c -> p a c", p=P)).then_inc(w_loaded, 16)
                sp.dma_start(room[:, 2560:3072].bitcast(U8).rearrange("p (a c) -> p a c", a=TT),
                             dram["mask_t"].rearrange("(a p) c -> p a c", p=P)).then_inc(w_loaded, 16)
                sp.dma_start(bqk[:, :, :], dram["b_qk"]).then_inc(w_loaded, 16)
                sp.dma_start(bv[:, :], dram["b_v"].partition_broadcast(P)).then_inc(w_loaded, 16)
                sp.dma_start(bo[:, :], dram["b_o"].partition_broadcast(P)).then_inc(w_loaded, 16)
                sp.dma_start(craw[:, :, :], dram["ctx_t"][0].rearrange("(a p) s -> p a s", p=P)).then_inc(c_loaded, 16)
                if router:
                    sp.dma_start(rw[:, :, :], dram["router_w"].rearrange("(k p) e -> p k e", p=P)).then_inc(w_loaded, 16)
                    sp.dma_start(rb[:, :], dram["router_b"].partition_broadcast(P)).then_inc(w_loaded, 16)
            else:
                for i in range(3):
                    sp.dma_start(room[:, i * 2048:(i + 1) * 2048].rearrange("p (a c) -> p a c", a=8),
                                 dram["down_t"][i].rearrange("(a p) c -> p a c", p=P)).then_inc(w_loaded, 16)
                sp.dma_start(room[:, 6144:6656].rearrange("p (a c) -> p a c", a=KT),
                             dram["wc"].rearrange("(a p) c -> p a c", p=P)).then_inc(w_loaded, 16)
                sp.dma_start(cosb[:, :], dram["cos"]).then_inc(w_loaded, 16)
                sp.dma_start(sinb[:, :], dram["sin"]).then_inc(w_loaded, 16)
                sp.wait_ge(consts, 1)
                for hh in range(2):
                    for i, (k, lo, n) in enumerate((("q_c", 0, 8), ("q_e", 8, 8), ("k_c", 0, 8), ("k_e", 8, 8), ("v_up", 0, 16))):
                        side = (0, 0, 1, 1, 2)[i]
                        sp.dma_start(up[hh * LAT:(hh + 1) * LAT, side, hh * DH + lo:hh * DH + lo + n],
                                     dram[k]).then_inc(w_loaded, 16)

            def stack(half):
                src = slice(half * 64, half * 64 + 64)
                for dst, side, parts in ((qst, 0, (qk_h, qk_h, qk_l)), (kst, 1, (qk_h, qk_l, qk_h))):
                    for term, part in enumerate(parts):
                        for t in range(2):
                            row = term * DH + t * 8
                            sp.dma_start(dst[row:row + 8, half, :, :].bitcast(F32),
                                         part[src, side, t, :].bitcast(F32)).then_inc(stacked[half], 16)

            if cross:
                sp.wait_ge(mask_chain, 8)
                sp.dma_start(kst[STACK:STACK + 1, :, :, :].rearrange("p a b s -> p (a b) s").bitcast(F32),
                             key_mask.unsqueeze(1).to_broadcast([1, H, S])).then_inc(key_row, 16)
            sp.wait_ge(consts, 2)
            sp.wait_ge(m_free, 6)
            sp.wait_ge(q_pool, POOL_TILES)
            stack(0)
            stack(1)

            def turn(t, steps):
                b, nxt, prev = t.b, t.has_next, t.has_prev
                if nxt:
                    if cross:
                        sp.wait_ge(ct_split, b + 1)
                        sp.sem_inc(held, 1)
                        sp.dma_start(craw[:, :, :], dram["ctx_t"][b + 1].rearrange("(a p) s -> p a s", p=P)).then_inc(c_loaded, 16)
                    sp.wait_ge(m_free, t.m + (m_index(steps, ("qk", 1, 0)) + 1))
                    sp.sem_inc(held, 1)
                    sp.wait_ge(q_pool, b * POOL_TILES + 2 * POOL_TILES)
                    sp.sem_inc(held, 1)
                    sp.wait_ge(st_ready, t.st + 2 * 16)
                    sp.sem_inc(held, 1)
                    stack(0)
                if prev:
                    sp.wait_ge(m_free, t.m + (m_index(steps, ("y", 1, -1)) + 1))
                    sp.sem_inc(held, 1)
                    sp.dma_start(x_out_v[b - 1], xres[:, :, :]).then_inc(stored, 16)
                    if router:
                        sp.wait_ge(xn3_ready, b * 1)
                        sp.sem_inc(held, 1)
                        sp.dma_start(table_v[b - 1][:, :, 0:C], xn[:, :, :]).then_inc(rows_stored, 16)
                        sp.wait_ge(rows_stored, b * 16)
                        sp.sem_inc(held, 1)
                    sp.wait_ge(stored, b * 16)
                    sp.sem_inc(held, 1)
                sp.dma_start(xres[:, :, :], x_in_v[b]).then_inc(xres_loaded, 16)
                if nxt:
                    sp.wait_ge(st_ready, t.st + 4 * 16)
                    sp.sem_inc(held, 1)
                    stack(1)
                else:
                    sp.wait_ge(m_free, t.m + (m_index(steps, ("y", 1, 0)) + 1))
                    sp.dma_start(x_out_v[b], xres[:, :, :]).then_inc(stored, 16)
                    if router:
                        sp.wait_ge(xn3_ready, B)
                        sp.dma_start(table_v[b][:, :, 0:C], xn[:, :, :]).then_inc(rows_stored, 16)
                        sp.wait_ge(rows_stored, B * 16)
                    sp.wait_ge(stored, B * 16)

            schedule.turns(sp, turn)

        @block.gpsimd
        def _(pool):
            nc.gpsimd.dma_start(xin[:, :, :], x_in_v[0]).then_inc(x_loaded, 16)
            n = [0]

            def fill(*ops):
                for op in ops:
                    n[0] += 1
                    op().then_inc(pool_chain, 1)
                    pool.wait_ge(pool_chain, n[0])

            if not cross:
                fill(lambda: nc.gpsimd.memset(up[:, :, :], 0.0))
                pool.sem_inc(consts, 1)
                fill(lambda: nc.gpsimd.memset(lower[:, :], 0.0),
                     lambda: nc.gpsimd.affine_select(out=lower[:, S - P:S], in_=lower[:, S - P:S], compare_op=ALU.is_ge,
                                                     fill=-BIG, base=0, pattern=[[-1, P]], channel_multiplier=1),
                     lambda: nc.gpsimd.memset(lower_t[:, :], 0.0),
                     lambda: nc.gpsimd.affine_select(out=lower_t[:, :], in_=lower_t[:, :], compare_op=ALU.is_ge,
                                                     fill=-BIG, base=0, pattern=[[1, P]], channel_multiplier=-1))
            else:
                pool.sem_inc(consts, 1)
            fill(lambda: nc.gpsimd.memset(half_neg[:, :], -0.5))
            if not cross:
                fill(lambda: nc.gpsimd.memset(vals[:, :, :, :], 0.0),
                     lambda: nc.gpsimd.memset(vals[:, :, :, DH:DH + 1], 1.0))
            CHAIN0 = n[0]

            def layernorm(x, done, chain):
                v, y, a, m = (lnw[:, i, :] for i in range(4))
                seq = (
                    lambda: nc.gpsimd.tensor_scalar(out=v, in0=mv[:, :, 1], scalar1=1.0, scalar2=EPS, op0=ALU.mult, op1=ALU.add),
                    lambda: nc.gpsimd.tensor_tensor(out=y, in0=v, in1=half_neg[:, :], op=ALU.pow),
                    lambda: nc.gpsimd.tensor_tensor(out=a, in0=y, in1=y, op=ALU.mult),
                    lambda: nc.gpsimd.tensor_tensor(out=a, in0=a, in1=v, op=ALU.mult),
                    lambda: nc.gpsimd.tensor_scalar(out=a, in0=a, scalar1=-0.5, scalar2=1.5, op0=ALU.mult, op1=ALU.add),
                    lambda: nc.gpsimd.tensor_tensor(out=y, in0=y, in1=a, op=ALU.mult),
                    lambda: nc.gpsimd.tensor_tensor(out=m, in0=mv[:, :, 0], in1=y, op=ALU.mult),
                    lambda: nc.gpsimd.tensor_scalar(out=m, in0=m, scalar1=-1.0, scalar2=0.0, op0=ALU.mult, op1=ALU.add),
                )
                for i, op in enumerate(seq):
                    op().then_inc(pool_chain, 1)
                    pool.wait_ge(pool_chain, chain + (i + 1))
                    pool.sem_inc(held, 1)
                for t in range(TT):
                    last = nc.gpsimd.tensor_scalar(out=xn[:, t, :], in0=x[:, t, :], scalar1=y[:, t:t + 1],
                                                   scalar2=m[:, t:t + 1], op0=ALU.mult, op1=ALU.add)
                last.then_inc(done, 1)

            LN_CHAIN = 8
            TILE_CHAIN = 1 if cross else 3

            def chain_of(steps):
                return (LN_CHAIN * count(steps, ("ln", "ln3")) + (count(steps, ("xt",)) // 2 if cross else 0) +
                        TILE_CHAIN * (count(steps, ("qk",)) // 2))


            def split_context(chain):
                nc.gpsimd.tensor_scalar(out=ct_h[:, :, :], in0=craw[:, :, :], scalar1=1.0, scalar2=0.0,
                                        op0=ALU.mult, op1=ALU.add).then_inc(pool_chain, 1)
                pool.wait_ge(pool_chain, chain + 1)
                nc.gpsimd.tensor_tensor(out=ct_l[:, :, :], in0=craw[:, :, :], in1=ct_h[:, :, :].bitcast(F32),
                                        op=ALU.subtract).then_inc(ct_split, 1)

            def finish_tile(side, t, chain):
                if cross:
                    src = qtmp[:, :]
                    done = 0
                else:
                    nc.gpsimd.tensor_tensor(out=rope_b[:, :], in0=rope_b[:, :], in1=sinb[:, :], op=ALU.mult).then_inc(pool_chain, 1)
                    pool.wait_ge(pool_chain, chain + 1)
                    nc.gpsimd.tensor_tensor(out=rope_a[:, :], in0=rope_a[:, :], in1=rope_b[:, :], op=ALU.add).then_inc(pool_chain, 1)
                    pool.wait_ge(pool_chain, chain + 2)
                    pool.sem_inc(held, 1)
                    src = rope_a[:, :]
                    done = 2
                nc.gpsimd.tensor_scalar(out=qk_h[:, side, t, :], in0=src, scalar1=1.0, scalar2=0.0,
                                        op0=ALU.mult, op1=ALU.add).then_inc(pool_chain, 1)
                pool.wait_ge(pool_chain, chain + (done + 1))
                nc.gpsimd.tensor_tensor(out=qk_l[:, side, t, :], in0=src, in1=qk_h[:, side, t, :].bitcast(F32),
                                        op=ALU.subtract).then_inc(q_pool, 1)
                return done + 1

            def run(t, steps, done=0):
                chain = schedule.before(t.b, chain_of) + CHAIN0 + done
                done = 0
                if t.loads:
                    pool.wait_ge(xn_ready, t.b + 1)
                    pool.sem_inc(held, 1)
                    nc.gpsimd.dma_start(xin[:, :, :], x_in_v[t.b + 1]).then_inc(x_loaded, 16)
                for s in steps:
                    if s[0] == "ln":
                        pool.wait_ge(stats_ready, t.nxt + 1)
                        if t.b is not None:
                            pool.wait_ge(m_ready, t.m)
                        pool.sem_inc(held, 1)
                        layernorm(xin, xn_ready, chain + done)
                        done += LN_CHAIN
                    if s[0] == "ln3":
                        pool.wait_ge(stats3_ready, t.b + (s[1] + 1))
                        pool.sem_inc(held, 1)
                        layernorm(xres, xn3_ready, chain + done)
                        done += LN_CHAIN
                    if s == ("xt", 0) and cross:
                        pool.wait_ge(c_loaded, t.nxt * 16 + 16)
                        if t.b is not None:
                            pool.wait_ge(m_ready, t.m + (m_index(steps, ("v", 1)) + 1))
                        pool.sem_inc(held, 1)
                        split_context(chain + done)
                        done += 1
                    if s[0] == "qk" and (s[1] == 0 if cross else s[2] == 1):
                        pool.wait_ge(m_free, t.m + (m_index(steps, s) + 1))
                        if t.b is not None:
                            pool.wait_ge(stacked[0], t.nxt * (16 * STACK_DMAS))
                            pool.wait_ge(stacked[1], t.nxt * (16 * STACK_DMAS))
                        pool.sem_inc(held, 1)
                        done += finish_tile(s[1], s[2], chain + done)
                    if s[0] == "mt":
                        pool.wait_ge(m_free, t.m + (m_index(steps, s) + 1))
                        pool.sem_inc(held, 1)
                        g = s[1] % GROUPS
                        nc.gpsimd.dma_start(qst[MAXROW:MAXROW + 2, g // 2, (g % 2) * GH:(g % 2 + 1) * GH, :].bitcast(F32),
                                            shift[:, :].bitcast(F32)).then_inc(shifted, 16)
                    if s[0] == "bias" and cross:
                        pool.wait_ge(xres_loaded, t.b * 16 + 16)
                        pool.sem_inc(held, 1)
                        for tt in range(TT):
                            last = nc.gpsimd.tensor_tensor(out=xres[:, tt, :], in0=xres[:, tt, :], in1=bo[:, :], op=ALU.add)
                        last.then_inc(res_bias, 1)
                assert done == chain_of(steps)

            start = Turn(schedule, None, schedule.first)
            run(start, schedule.first[:1])
            if not cross:
                pool.wait_ge(xn_ready, 1)
                for i, rows in enumerate((qst, kst)):
                    nc.gpsimd.memset(rows[MAXROW:P, :, :, :].bitcast(F32), 1.0).then_inc(ones_ready, 1)
                    pool.wait_ge(ones_ready, i + 1)
            pool.wait_ge(prep_dve, 1)
            pool.sem_inc(consts, 1)
            if cross:
                pool.wait_ge(w_loaded, 16 * (11 if router else 9))
            run(start, schedule.first[1:], LN_CHAIN)
            schedule.turns(pool, run)

        @block.tensor
        def _(pe):
            if not cross:
                pe.wait_ge(w_loaded, 16 * 16)
                for i, bank in enumerate((ps_p1[:, 0, :], ps_p1[:, 1, :], ps_st[:, 0, :])):
                    for ct in range(KT):
                        for pair in range(8):
                            at = ct * C + pair * 32
                            last = nc.tensor.matmul(bank[:, at:at + 32],
                                                    room[:, i * 2048 + pair * C + ct * P:i * 2048 + pair * C + ct * P + P],
                                                    up[:, i, :], start=True, stop=True)
                    last.then_inc(prep_mm, 1)
            else:
                pe.wait_ge(prep_dve, 2)
                for kt in range(TT):
                    last = nc.tensor.matmul(ps_p1[:, 0, :], ones[:, :], lower_t[:, kt, :], start=(kt == 0), stop=(kt == TT - 1))
                last.then_inc(prep_mm, 1)
                pe.wait_ge(mask_chain, 3)
                nc.tensor.matmul(ps_p1[:, 1, 0:TT], ones[:, :], differs, start=True, stop=True).then_inc(prep_mm, 1)
                pe.wait_ge(mask_chain, 7)
                for kt in range(TT):
                    last = nc.tensor.matmul(ps_p1[:, 0, kt * P:(kt + 1) * P], key_cols[:, kt, :], identb[:, :], start=True, stop=True)
                last.then_inc(prep_mm, 1)

            def three(out, w, wsl, x_h, x_l, xsl, x_first):
                n = 0
                for kt in range(KT):
                    for wp, xp in ((0, x_h), (0, x_l), (1, x_h)):
                        a, c = w(wp, kt)[:, wsl], xp[:, kt, xsl]
                        last = nc.tensor.matmul(out, c if x_first else a, a if x_first else c,
                                                start=(n == 0), stop=(n == 3 * KT - 1))
                        n += 1
                return last

            def run(t, steps):
                m, p1, st = 0, 0, 0
                for s in steps:
                    kind = s[0]
                    if kind in M_KINDS:
                        bank = ps_m[:, (t.m_par + m) % 2, :]
                        if not (t.b is None and m < 2):
                            pe.wait_ge(m_free, t.m + (m - 1))
                    if kind == "xt":
                        if s[1] == 0:
                            pe.wait_ge(xn_ready, t.nxt + 1)
                        for tt in range(TT):
                            last = nc.tensor.transpose(bank[:, tt * P:(tt + 1) * P], xn[:, tt, s[1] * P:(s[1] + 1) * P], ident[:, :])
                    elif kind == "xt3":
                        if s[1] == 0:
                            pe.wait_ge(xn3_ready, t.b + (s[2] + 1))
                        for tt in range(TT):
                            last = nc.tensor.transpose(bank[:, tt * P:(tt + 1) * P], xn[:, tt, s[1] * P:(s[1] + 1) * P], ident[:, :])
                    elif kind == "lg":
                        pe.wait_ge(m_free, t.m + (m_index(steps, ("xt3", 1, s[2])) + 1))
                        for i in range(2):
                            at = slice((2 * s[1] + i) * P, (2 * s[1] + i + 1) * P)
                            for k in range(KT):
                                last = nc.tensor.matmul(bank[:, i * E_N:(i + 1) * E_N], xnt[:, k, at], rw[:, k, :],
                                                        start=(k == 0), stop=(k == KT - 1))
                    elif kind == "qk":
                        side, tile = s[1:]
                        if (side, tile) == (0, 1):
                            pe.wait_ge(m_free, t.m + (m_index(steps, ("xt", 1)) + 1))
                        if cross and (side, tile) == (1, 1):
                            pe.wait_ge(ct_split, t.nxt + 1)
                        src_h, src_l = (ct_h, ct_l) if cross and side else (xt_h, xt_l)
                        last = three(bank, lambda p, k: wqk[:, p, side, k, :], slice(tile * P, (tile + 1) * P),
                                     src_h, src_l, slice(0, S), False)
                    elif kind == "v":
                        src_h, src_l = (ct_h, ct_l) if cross else (xt_h, xt_l)
                        for i in range(2):
                            tt = 2 * s[1] + i
                            last = three(bank[:, i * C:(i + 1) * C], lambda p, k: wv[:, p, k, :], slice(0, C),
                                         src_h, src_l, slice(tt * P, (tt + 1) * P), True)
                    elif kind == "p1":
                        g, j, qt = s[1] % GROUPS, s[2], s[3]
                        if g % 2 == 0 and j == 0 and qt == 0:
                            batch = t.nxt if s[1] >= GROUPS else t.b
                            pe.wait_ge(stacked[g // 2], batch * (16 * STACK_DMAS) + 16 * STACK_DMAS)
                        if not (t.b is None and p1 < 2):
                            pe.wait_ge(max_done, t.p1 + (p1 - 1))
                        hh = (g % 2) * GH + j
                        last = nc.tensor.matmul(ps_p1[:, (t.p1_par + p1) % 2, 0:keys_of(qt)],
                                                qst[0:MAXROW, g // 2, hh, qt * P:(qt + 1) * P],
                                                kst[0:MAXROW, g // 2, hh, 0:keys_of(qt)], start=True, stop=True)
                        last.then_inc(p1_ready, 1)
                        p1 += 1
                    elif kind == "mt":
                        k = s[1] if t.b is not None else 0
                        pe.wait_ge(neg_ready, (0 if t.b is None else t.b * GROUPS) + (k + 1))
                        last = nc.tensor.transpose(bank[0:32, 0:P], neg[:, :, :].rearrange("p a b -> p (a b)").bitcast(F32), ident[:, :])
                    elif kind == "st":
                        g, kt, j = s[1:]
                        if kt == 0 and j == 0:
                            pe.wait_ge(shifted, t.b * (16 * GROUPS) + 16 * (g + 1))
                        pe.wait_ge(exp_done, t.st + (st + 1))
                        hh = (g % 2) * GH + j
                        lo = width(kt)
                        out = ps_st[:, st % 2, 0:S - lo]
                        rows = STACK + 1 if cross else STACK
                        last = nc.tensor.matmul(out, kst[0:rows, g // 2, hh, kt * P:(kt + 1) * P],
                                                qst[0:rows, g // 2, hh, lo:S], start=True, stop=not masked)
                        if cross and masked:
                            last = nc.tensor.matmul(out, identb[:, :], lower_t[:, kt, :], start=False, stop=True)
                        elif masked:
                            last = nc.tensor.matmul(ps_st[:, st % 2, 0:P], identb[:, :], lower_t[:, :], start=False, stop=True)
                        last.then_inc(st_ready, 1)
                        st += 1
                    elif kind == "pv":
                        g, kt, j = s[1:]
                        lo = width(kt)
                        if g == 0 and j == 0 and kt % 2 == 0:
                            pe.wait_ge(m_free, t.m + (m_index(steps, ("v", kt // 2)) + 1))
                        if kt == 0 and j == 0:
                            pe.wait_ge(o_raw, t.b * GROUPS + (g + 1))
                        if j == 0:
                            pe.wait_ge(exp_done, t.st + (16 * g + 4 * kt + 4 + 2))
                        last = nc.tensor.matmul(ps_o[32 * j:32 * j + 32, g % 2, lo:S], vals[:, kt, GH * (g % GROUPS) + j, :],
                                                probs[:, kt, j, 0:S - lo], start=(kt == 0), stop=(kt == TT - 1))
                        if kt == TT - 1 and j == GH - 1:
                            last.then_inc(pv_done, 1)
                    elif kind == "og":
                        g = s[1]
                        pe.wait_ge(o_raw, t.b * GROUPS + (g + 3))
                        for qt in range(TT):
                            last = nc.tensor.transpose(bank[:, qt * P:(qt + 1) * P], oraw[:, g % 2, qt * P:(qt + 1) * P], ident[:, :])
                    elif kind == "ot":
                        pe.wait_ge(m_free, t.m + (m_index(steps, ("og", 3 + 4 * s[2])) + 1))
                        for qt in range(TT):
                            last = nc.tensor.transpose(bank[:, qt * P:(qt + 1) * P], ocomp[:, qt, s[1] * P:(s[1] + 1) * P], ident[:, :])
                    elif kind == "y":
                        pe.wait_ge(m_free, t.m + (m_index(steps, ("ot", 1, s[2])) + 1))
                        for i in range(2):
                            tt = 2 * s[1] + i
                            last = three(bank[:, i * C:(i + 1) * C], lambda p, k: wo[:, p, k, :], slice(0, C),
                                         ot_h, ot_l, slice(tt * P, (tt + 1) * P), True)
                    if kind in M_KINDS:
                        last.then_inc(m_ready, 1)
                        m += 1

            pe.wait_ge(prep_dve, 4)
            pe.wait_ge(prep_act, 1)
            pe.wait_ge(consts, 2)
            masked = not cross
            run(Turn(schedule, None, schedule.first), schedule.first)
            if not cross:
                schedule.turns(pe, run)
            else:
                varies = pe.value_load(vary[0:1, 0:1], min_val=0, max_val=1)
                pe.wait_ge(key_row, 16)
                with pe.If(varies == 0):
                    schedule.turns(pe, run)
                masked = True
                with pe.If(varies != 0):
                    schedule.turns(pe, run)

        def head_order(m, tile):
            return m.rearrange("p (t m d j) -> p t m j d", t=2, m=2, d=8)[:, tile, :, :, :]

        @block.scalar
        def _(act):
            act.sem_inc(exp_done, 2)
            act.sem_inc(o_raw, 2)
            if cross:
                act.wait_ge(w_loaded, 16 * (11 if router else 9))
                for i, dst in enumerate((wqk[:, 0, 0], wqk[:, 0, 1], wv[:, 0], wo[:, 0])):
                    last = nc.scalar.activation(dst, room[:, i * 512:(i + 1) * 512].rearrange("p (a c) -> p a c", a=KT), ACT.Copy)
            else:
                act.wait_ge(prep_mm, 3)
                for side in range(2):
                    for ct in range(KT):
                        for tile in range(2):
                            src = ps_p1[:, side, ct * C:(ct + 1) * C].rearrange("p (m j t d) -> p t m j d", m=2, j=8, t=2)[:, tile]
                            nc.scalar.activation(head_order(wqk[:, 0, side, ct, :], tile), src, ACT.Copy)
                nc.scalar.activation(wv[:, 0, :, :], ps_st[:, 0, :].rearrange("p (a c) -> p a c", a=KT), ACT.Copy)
                act.wait_ge(w_loaded, 16 * 16)
                last = nc.scalar.activation(wo[:, 0, :, :], room[:, 6144:6656].rearrange("p (a c) -> p a c", a=KT), ACT.Copy)
            last.then_inc(prep_act, 1)
            act.wait_ge(prep_dve, 4)
            act.wait_ge(consts, 2)

            def run(t, steps):
                m, st, hd = 0, 0, 0
                for s in steps:
                    kind = s[0]
                    if kind in H_KINDS and not (kind == "qk" and (s[1] == 0 if cross else s[2] == 1)):
                        bank = ps_m[:, (t.m_par + m) % 2, :]
                        act.wait_ge(m_ready, t.m + (m + 1))
                        if kind == "xt":
                            nc.scalar.activation(xt_h[:, s[1], :], bank, ACT.Copy).then_inc(h_done, 1)
                        elif kind == "ot":
                            nc.scalar.activation(ot_h[:, s[1], :], bank, ACT.Copy).then_inc(h_done, 1)
                        else:
                            if t.b is not None:
                                act.wait_ge(stacked[0], t.nxt * (16 * STACK_DMAS))
                                act.wait_ge(stacked[1], t.nxt * (16 * STACK_DMAS))
                            if cross:
                                nc.scalar.activation(qk_h[:, s[1], s[2], :], bank, ACT.Identity, bias=bqk[:, s[1], s[2]:s[2] + 1]).then_inc(h_done, 1)
                            else:
                                nc.scalar.activation(qk_h[:, s[1], s[2], :], bank, ACT.Copy).then_inc(h_done, 1)
                    if kind in M_KINDS:
                        m += 1
                    if kind == "st":
                        g, kt, j = s[1:]
                        n = S - width(kt)
                        act.wait_ge(st_ready, t.st + (st + 1))
                        nc.scalar.activation(probs[:, kt, j, 0:n], ps_st[:, st % 2, 0:n], ACT.Exp,
                                             scale=float(DH) ** -0.5).then_inc(exp_done, 1)
                        st += 1
                    if kind == "pv" and s[2:] == (TT - 1, GH - 1):
                        g = s[1]
                        act.wait_ge(pv_done, t.b * GROUPS + (g + 1))
                        nc.scalar.activation(oraw[:, g % 2, :], ps_o[:, g % 2, :], ACT.Copy).then_inc(o_raw, 1)

            run(Turn(schedule, None, schedule.first), schedule.first)
            schedule.turns(act, run)

        @block.vector
        def _(dve):
            def high_first(s):
                return s[0] in H_KINDS and not (s[0] == "qk" and (s[1] == 0 if cross else s[2] == 1))

            def run(t, steps, chain=0):
                m, p1, hd, tiles = 0, 0, 0, 0
                c0 = schedule.before(t.b, lambda x: count(x, ("ln", "ln3", "neg", "og")))
                mb = schedule.before(t.b, lambda x: sum(high_first(s) for s in x))
                for s in steps:
                    kind = s[0]
                    if kind in ("ln", "ln3"):
                        src, done = (xin, stats_ready) if kind == "ln" else (xres, stats3_ready)
                        if kind == "ln":
                            dve.wait_ge(x_loaded, t.nxt * 16 + 16)
                        else:
                            dve.wait_ge(m_free, t.m + m)
                            if t.has_next:
                                dve.wait_ge(xn_ready, t.nxt + 1)
                            else:
                                dve.wait_ge(xn_ready, B)
                                if s[1] == 0:
                                    dve.wait_ge(xn3_ready, B - 1)
                        if kind == "ln" and t.b is not None:
                            dve.wait_ge(xn_ready, t.nxt)
                            if router and t.has_prev:
                                dve.wait_ge(xres_loaded, t.b * 16)
                        for tt in range(TT):
                            last = nc.vector.bn_stats(stats[:, tt, :], src[:, tt, :])
                        last.then_inc(dve_chain, 1)
                        chain += 1
                        dve.wait_ge(dve_chain, c0 + chain)
                        dve.sem_inc(held, 1)
                        for tt in range(TT):
                            last = nc.vector.bn_aggr(mv[:, tt, :], stats[:, tt, :])
                        last.then_inc(done, 1)
                    if kind == "p1":
                        g, j, qt = s[1], s[2], s[3]
                        n = keys_of(qt)
                        add = lower[:, qt, :] if cross else lower[:, S - n:S]
                        dve.wait_ge(p1_ready, t.p1 + (p1 + 1))
                        dve.sem_inc(held, 1)
                        bank = ps_p1[:, (t.p1_par + p1) % 2, 0:n]
                        nc.vector.tensor_tensor_reduce(out=bank, in0=bank, in1=add,
                                                       scale=1.0, scalar=-3.0e38, op0=ALU.add, op1=ALU.max,
                                                       accum_out=mx[:, g % 2, j * TT + qt:j * TT + qt + 1]).then_inc(max_done, 1)
                        p1 += 1
                    elif kind == "neg":
                        g = s[1] % 2
                        dve.wait_ge(max_done, t.p1 + p1)
                        nc.vector.tensor_scalar(out=neg[:, 0, :], in0=mx[:, g, :], scalar1=-1.0, scalar2=None,
                                                op0=ALU.mult).then_inc(dve_chain, 1)
                        chain += 1
                        dve.wait_ge(dve_chain, c0 + chain)
                        nc.vector.scalar_tensor_tensor(out=neg[:, 1, :], in0=mx[:, g, :], scalar=-1.0, in1=neg[:, 0, :].bitcast(F32),
                                                       op0=ALU.mult, op1=ALU.subtract).then_inc(neg_ready, 1)
                    if kind not in M_KINDS:
                        continue
                    bank = ps_m[:, (t.m_par + m) % 2, :]
                    dve.wait_ge(m_ready, t.m + (m + 1))
                    m += 1
                    pooled = kind == "qk" and (s[1] == 0 if cross else s[2] == 1)
                    if kind in H_KINDS and not pooled:
                        hd += 1
                        dve.wait_ge(h_done, mb + hd)
                    if kind in ("xt", "ot"):
                        hi, lo = (xt_h, xt_l) if kind == "xt" else (ot_h, ot_l)
                        nc.vector.tensor_tensor(out=lo[:, s[1], :], in0=bank, in1=hi[:, s[1], :].bitcast(F32),
                                                op=ALU.subtract).then_inc(m_free, 1)
                    elif kind == "qk" and pooled:
                        if not (t.b is None and tiles == 0):
                            dve.wait_ge(q_pool, t.nxt * POOL_TILES + tiles)
                        tiles += 1
                        if cross:
                            nc.vector.scalar_tensor_tensor(out=qtmp[:, :], in0=bank, scalar=bqk[:, s[1], s[2]:s[2] + 1],
                                                           in1=some_key[:, :], op0=ALU.add, op1=ALU.mult).then_inc(m_free, 1)
                        else:
                            nc.vector.tensor_tensor(out=rope_a[:, :], in0=bank, in1=cosb[:, :], op=ALU.mult)
                            nc.vector.stream_shuffle(rope_b[:, :], bank, [i ^ 8 for i in range(32)]).then_inc(m_free, 1)
                    elif kind == "qk":
                        if cross:
                            nc.vector.scalar_tensor_tensor(out=qk_l[:, s[1], s[2], :], in0=bank, scalar=bqk[:, s[1], s[2]:s[2] + 1],
                                                           in1=qk_h[:, s[1], s[2], :].bitcast(F32), op0=ALU.add,
                                                           op1=ALU.subtract).then_inc(m_free, 1)
                        else:
                            nc.vector.tensor_tensor(out=qk_l[:, s[1], s[2], :], in0=bank, in1=qk_h[:, s[1], s[2], :].bitcast(F32),
                                                    op=ALU.subtract).then_inc(m_free, 1)
                    elif kind == "v":
                        for i in range(2):
                            out = vals[:, 2 * s[1] + i, :, 0:DH]
                            src = bank[:, i * C:(i + 1) * C].rearrange("p (h d) -> p h d", h=H)
                            if cross:
                                last = nc.vector.tensor_tensor(out=out, in0=src, in1=bv[:, :].rearrange("p (h d) -> p h d", h=H), op=ALU.add)
                            else:
                                last = nc.vector.tensor_copy(out, src)
                        last.then_inc(m_free, 1)
                    elif kind == "xt3":
                        nc.vector.tensor_copy(xnt[:, s[1], :], bank).then_inc(m_free, 1)
                    elif kind == "lg":
                        nc.vector.tensor_tensor(out=logits[:, bass.ds(t.b * TT + (s[2] * TT + 2 * s[1]), 2), :],
                                                in0=bank[:, 0:2 * E_N].rearrange("p (t e) -> p t e", e=E_N),
                                                in1=rb[:, :].unsqueeze(1).to_broadcast([P, 2, E_N]), op=ALU.add).then_inc(m_free, 1)
                    elif kind == "mt":
                        if t.b is not None:
                            dve.wait_ge(shifted, t.b * (16 * GROUPS) + 16 * s[1])
                        nc.vector.tensor_copy(shift[:, :], bank[0:32, 0:P]).then_inc(m_free, 1)
                    elif kind == "og":
                        g = s[1]
                        view = bank.rearrange("p (q d) -> p q d", d=32)
                        nc.vector.reciprocal(rec[:, g % 2, :], view[:, :, DH]).then_inc(dve_chain, 1)
                        chain += 1
                        dve.wait_ge(dve_chain, c0 + chain)
                        nc.vector.tensor_tensor(
                            out=ocomp[:, :, (g % GROUPS) * GH * DH:(g % GROUPS + 1) * GH * DH].rearrange("p q (j d) -> p q j d", d=DH),
                            in0=bank.rearrange("p (q j d) -> p q j d", q=TT, d=32)[:, :, :, 0:DH],
                            in1=rec[:, g % 2, :].rearrange("p (q j) -> p q j", q=TT).unsqueeze(3).to_broadcast([P, TT, GH, DH]),
                            op=ALU.mult).then_inc(m_free, 1)
                    elif kind == "y":
                        if s[1] == 0:
                            if cross:
                                dve.wait_ge(res_bias, t.b + (s[2] + 1))
                            else:
                                dve.wait_ge(xres_loaded, t.b * 16 + 16 * (s[2] + 1))
                        res = xres[:, 2 * s[1]:2 * s[1] + 2, :]
                        nc.vector.tensor_tensor(out=res, in0=bank.rearrange("p (i c) -> p i c", i=2), in1=res,
                                                op=ALU.add).then_inc(m_free, 1)

            start = Turn(schedule, None, schedule.first)
            run(start, schedule.first[:1])
            if not cross:
                nc.vector.memset(qst[0:MAXROW, :, :, :].bitcast(F32), 0.0)
                nc.vector.memset(kst[0:MAXROW, :, :, :].bitcast(F32), 0.0).then_inc(prep_dve, 1)
            else:
                dve.sem_inc(prep_dve, 1)
            if cross:
                dve.wait_ge(w_loaded, 16 * (11 if router else 9))
                nc.vector.tensor_scalar(out=lower[:, :, :], in0=room[:, 2048:2560].bitcast(U8).rearrange("p (a c) -> p a c", a=TT),
                                        scalar1=BIG, scalar2=-BIG, op0=ALU.mult, op1=ALU.add)
                nc.vector.memset(ones[:, :], 1.0)
                nc.vector.tensor_scalar(out=lower_t[:, :, :], in0=room[:, 2560:3072].bitcast(U8).rearrange("p (a c) -> p a c", a=TT),
                                        scalar1=1.0, scalar2=None, op0=ALU.mult).then_inc(prep_dve, 1)
                dve.wait_ge(prep_mm, 1)
                nc.vector.tensor_scalar(out=some_key[:, :], in0=ps_p1[:, 0, :], scalar1=1.0, scalar2=None, op0=ALU.min)
                nc.vector.tensor_scalar(out=lower_t[:, :, :], in0=room[:, 2560:3072].bitcast(U8).rearrange("p (a c) -> p a c", a=TT),
                                        scalar1=BIG, scalar2=-BIG, op0=ALU.mult, op1=ALU.add).then_inc(prep_dve, 1)
                def link(ins, n):
                    ins.then_inc(mask_chain, 1)
                    dve.wait_ge(mask_chain, n)

                dve.wait_ge(prep_dve, 3)
                link(nc.vector.tensor_reduce(keepers, lower_t[:, :, :], AX.X, ALU.max), 1)
                link(nc.vector.tensor_reduce(keep_all, lower_t[:, :, :], AX.X, ALU.min), 2)
                nc.vector.tensor_tensor(out=differs, in0=keepers, in1=keep_all, op=ALU.subtract).then_inc(mask_chain, 1)
                dve.wait_ge(prep_mm, 2)
                link(nc.vector.tensor_reduce(vary_sum, ps_p1[:, 1, 0:TT], AX.X, ALU.add), 4)
                link(nc.vector.tensor_scalar(out=vary[0:1, 0:1], in0=vary_sum[0:1, 0:1], scalar1=0.0, scalar2=None, op0=ALU.is_gt), 5)
                link(nc.vector.tensor_scalar(out=alike, in0=vary_sum, scalar1=0.0, scalar2=None, op0=ALU.is_equal), 6)
                nc.vector.tensor_tensor(out=key_cols, in0=keepers.unsqueeze(2).to_broadcast([P, TT, P]),
                                        in1=alike.unsqueeze(2).to_broadcast([P, TT, P]), op=ALU.mult).then_inc(mask_chain, 1)
                dve.wait_ge(prep_mm, 3)
                nc.vector.tensor_copy(key_mask, ps_p1[0:1, 0, :]).then_inc(mask_chain, 1)
                dve.wait_ge(prep_act, 1)
                for i, (hi, lo) in enumerate(((wqk[:, 0, 0], wqk[:, 1, 0]), (wqk[:, 0, 1], wqk[:, 1, 1]), (wv[:, 0], wv[:, 1]), (wo[:, 0], wo[:, 1]))):
                    last = nc.vector.tensor_tensor(out=lo, in0=room[:, i * 512:(i + 1) * 512].rearrange("p (a c) -> p a c", a=KT),
                                                   in1=hi.bitcast(F32), op=ALU.subtract)
                last.then_inc(prep_dve, 1)
            else:
                dve.wait_ge(prep_act, 1)
                for side in range(2):
                    for ct in range(KT):
                        for tile in range(2):
                            src = ps_p1[:, side, ct * C:(ct + 1) * C].rearrange("p (m j t d) -> p t m j d", m=2, j=8, t=2)[:, tile]
                            nc.vector.tensor_tensor(out=head_order(wqk[:, 1, side, ct, :], tile), in0=src,
                                                    in1=head_order(wqk[:, 0, side, ct, :], tile).bitcast(F32), op=ALU.subtract)
                nc.vector.tensor_tensor(out=wv[:, 1, :, :], in0=ps_st[:, 0, :].rearrange("p (a c) -> p a c", a=KT),
                                        in1=wv[:, 0, :, :].bitcast(F32), op=ALU.subtract)
                nc.vector.tensor_tensor(out=wo[:, 1, :, :], in0=room[:, 6144:6656].rearrange("p (a c) -> p a c", a=KT),
                                        in1=wo[:, 0, :, :].bitcast(F32), op=ALU.subtract).then_inc(prep_dve, 3)
            dve.wait_ge(consts, 2)

            run(start, schedule.first[1:], 1)
            schedule.turns(dve, run)


def mixture(nc, out, table, logits, dram, ident):
    ctx = ExitStack()
    with ctx:
        def sb(n, shape, dt):
            return ctx.enter_context(nc.sbuf_tensor(f"moe_{n}", shape, dt))

        def sem(n):
            return ctx.enter_context(nc.semaphore(f"moe_{n}"))

        FT = DFF // P
        CT = CAP // P
        HI, LO = 32, 16
        BITS, UNROLL = 30, 6
        SC = E_N * NT

        top = sb("top", [P, NT], F32)
        tot = sb("tot", [P, NT], F32)
        score = sb("score", [P, E_N, NT], F32)
        bit = sb("bit", [P, 2, E_N], I32)
        thr = sb("thr", [P, E_N], I32)
        cand = sb("cand", [P, E_N], I32)
        won = sb("won", [P, E_N], I32)
        ge = sb("ge", [P, E_N, NT], BF16)
        cnt = sb("cnt", [P, E_N], BF16)
        above = sb("above", [P, E_N, NT], BF16)
        tied = sb("tied", [P, E_N, NT], BF16)
        need = sb("need", [P, E_N], F32)
        scan = sb("scan", [P, SC], F32)
        restart = sb("restart", [P, E_N, NT], F32)
        rank = sb("rank", [P, SC], F32)
        picked = sb("picked", [P, E_N, NT], BF16)
        place = sb("place", [P, E_N, NT], I32)
        place_hi = sb("place_hi", [P, E_N, NT], I32)
        place_lo = sb("place_lo", [P, E_N, NT], I32)
        ones = sb("ones", [P, P], BF16)
        before = sb("before", [P, P], BF16)
        iota = sb("iota", [P, HI], I32)
        tile_no = sb("tile_no", [P, NT], I32)
        part_no = sb("part_no", [P, 1], F32)
        part_i = sb("part_i", [P, 1], I32)
        hot_hi = sb("hot_hi", [P, 2, NT, HI], BF16)
        hot_lo = sb("hot_lo", [P, 2, NT, LO], BF16)
        hot_id = sb("hot_id", [P, 2, NT, 2, LO], BF16)
        id_part = sb("id_part", [HI, 2, LO], F32)
        id_tok = sb("id_tok", [HI, 2, LO], I32)
        ids = sb("ids", [P, 2, CT], I32)
        w1r = sb("w1r", [P, 2, KT, DFF], F32)
        w2r = sb("w2r", [P, 2, FT, C], F32)
        w1 = sb("w1", [P, 2, 2, KT, DFF], F32R)
        w2 = sb("w2", [P, 2, 2, FT, C], F32R)
        b1 = sb("b1", [P, E_N, FT], F32)
        b2 = sb("b2", [P, E_N, C], F32)
        tok = sb("tok", [P, 2, CT, ROW], F32)
        tok_h = sb("tok_h", [P, 2, KT, CAP], F32R)
        tok_l = sb("tok_l", [P, 2, KT, CAP], F32R)
        relu = sb("relu", [P, 2, CAP], F32)
        hid_h = sb("hid_h", [P, 4, CAP], F32R)
        hid_l = sb("hid_l", [P, 4, CAP], F32R)
        part = sb("part", [P, CT, C], F32)

        ps_a = ctx.enter_context(nc.psum_tensor("moe_ps_a", [P, 2, S], F32))
        ps_h = ctx.enter_context(nc.psum_tensor("moe_ps_h", [P, 2, S], F32))
        ps_y = ctx.enter_context(nc.psum_tensor("moe_ps_y", [P, CT, S], F32))

        held = sem("held")
        in_loaded = sem("in_loaded")
        consts = sem("consts")
        pool_chain = sem("pool_chain")
        dve_chain = sem("dve_chain")
        scores_stored = sem("scores_stored")
        scored = sem("scored")
        exp_in = sem("exp_in")
        exp_out = sem("exp_out")
        cnt_ready = sem("cnt_ready")
        cnt_sum = sem("cnt_sum")
        pre_in = sem("pre_in")
        pre_out = sem("pre_out")
        hot_ready = sem("hot_ready")
        id_sum = sem("id_sum")
        id_free = sem("id_free")
        id_ready = sem("id_ready")
        ids_moved = sem("ids_moved")
        gathered = sem("gathered")
        w_loaded = [sem(f"w_loaded_{q}") for q in range(2)]
        w_high = sem("w_high")
        w1_low = sem("w1_low")
        w2_low = sem("w2_low")
        t_ready = sem("t_ready")
        t_high = sem("t_high")
        t_free = sem("t_free")
        g_ready = sem("g_ready")
        relu_done = sem("relu_done")
        hid_high = sem("hid_high")
        hid_low = sem("hid_low")
        y_ready = sem("y_ready")
        y_free = sem("y_free")
        weighted = sem("weighted")
        scattered = sem("scattered")
        part_free = sem("part_free")

        block = ctx.enter_context(nc.Block())

        @block.sync
        def _(sp):
            sp.dma_start(b1[:, :, :], dram["b1"]).then_inc(in_loaded, 16)
            sp.dma_start(b2[:, :, :], dram["b2"].partition_broadcast(P)).then_inc(in_loaded, 16)
            def weights(e, q):
                sp.dma_start(w1r[:, q, :, :], dram["w1"][e].rearrange("(k p) f -> p k f", p=P)).then_inc(w_loaded[q], 16)
                sp.dma_start(w2r[:, q, :, :], dram["w2"][e].rearrange("(k p) f -> p k f", p=P)).then_inc(w_loaded[q], 16)

            weights(0, 0)
            weights(1, 1)
            sp.wait_ge(scored, 1)
            with nc.allow_non_contiguous_dma(reason="8 scores of a row"):
                sp.dma_start(table.rearrange("(t p) c -> p t c", p=P)[:, :, C:C + E_N], logits[:, :, :]).then_inc(scores_stored, 16)

            def listed(e, q):
                sp.wait_ge(id_ready, e + 1)
                sp.sem_inc(held, 1)
                sp.dma_start(ids[:, q, :], id_tok[:, q, :]).then_inc(ids_moved, 16)

            def expert(e, q, nxt, more):
                if nxt:
                    sp.wait_ge(part_free, e + 1)
                    sp.sem_inc(held, 1)
                    listed(e + 1, 1 - q)
                if more:
                    sp.wait_ge(w_high, e * 4 + 4)
                    sp.sem_inc(held, 1)
                    sp.wait_ge(w1_low, e + 1)
                    sp.sem_inc(held, 1)
                    sp.wait_ge(w2_low, e * 2 + 2)
                    sp.sem_inc(held, 1)
                    weights(e + 2, q)

            listed(0, 0)
            with sp.Fori(0, E_N // 2 - 1) as i:
                for q in range(2):
                    expert(i * 2 + q, q, True, True)
            expert(E_N - 2, 0, True, False)

        @block.gpsimd
        def _(pool):
            n = 0
            for op in (
                lambda: nc.gpsimd.memset(ones[:, :], 1.0),
                lambda: nc.gpsimd.memset(before[:, :], 1.0),
                lambda: nc.gpsimd.affine_select(out=before[:, :], in_=before[:, :], compare_op=ALU.is_gt, fill=0.0,
                                                base=0, pattern=[[1, P]], channel_multiplier=-1),
                lambda: nc.gpsimd.iota(iota[:, :], pattern=[[1, HI]], base=0, channel_multiplier=0),
                lambda: nc.gpsimd.iota(tile_no[:, :], pattern=[[1, NT]], base=0, channel_multiplier=0),
                lambda: nc.gpsimd.iota(part_i[:, :], pattern=[[1, 1]], base=0, channel_multiplier=1),
                lambda: nc.gpsimd.tensor_copy(part_no[:, :], part_i[:, :]),
                lambda: nc.gpsimd.memset(restart[:, :, :], 1.0),
                lambda: nc.gpsimd.memset(restart[:, :, 0:1], 0.0),
            ):
                n += 1
                op().then_inc(pool_chain, 1)
                pool.wait_ge(pool_chain, n)
            pool.sem_inc(consts, 1)

            pool.sem_inc(part_free, 1)

            def low_w1(e, q):
                pool.wait_ge(w_high, e * 4 + 2)
                nc.gpsimd.tensor_tensor(out=w1[:, q, 1, :, :], in0=w1r[:, q, :, :], in1=w1[:, q, 0, :, :].bitcast(F32),
                                        op=ALU.subtract).then_inc(w1_low, 1)

            def gather(e, q):
                pool.wait_ge(ids_moved, e * 16 + 16)
                pool.sem_inc(held, 1)
                for c in range(CT):
                    nc.gpsimd.indirect_dma_start(out=tok[:, q, c, :], out_offset=None, in_=table[:, :],
                                                 in_offset=bass.IndirectOffsetOnAxis(ap=ids[:, q, c:c + 1], axis=0)
                                                 ).then_inc(gathered, 16)

            def scatter(e, q):
                for c in range(CT):
                    pool.wait_ge(weighted, e * CT + (c + 1))
                    pool.sem_inc(held, 1)
                    nc.gpsimd.indirect_dma_start(out=out[:, :], out_offset=bass.IndirectOffsetOnAxis(ap=ids[:, q, c:c + 1], axis=0),
                                                 in_=part[:, c, :], in_offset=None, compute_op=ALU.add).then_inc(scattered, 16)

            low_w1(0, 0)
            pool.wait_ge(scores_stored, 16)
            gather(0, 0)

            def expert(e, q, nxt):
                if nxt:
                    gather(e + 1, 1 - q)
                    low_w1(e + 1, 1 - q)
                scatter(e, q)
                pool.wait_ge(scattered, e * (16 * CT) + 16 * CT)
                pool.sem_inc(part_free, 1)

            with pool.Fori(0, E_N // 2 - 1) as i:
                for q in range(2):
                    expert(i * 2 + q, q, True)
            expert(E_N - 2, 0, True)
            expert(E_N - 1, 1, False)

        @block.tensor
        def _(pe):
            pe.wait_ge(consts, 1)

            def totals(k):
                pe.wait_ge(cnt_ready, k)
                nc.tensor.matmul(ps_h[:, 0, 0:E_N], ones[:, :], cnt[:, :], start=True, stop=True).then_inc(cnt_sum, 1)

            with pe.Fori(0, BITS // UNROLL) as i:
                for u in range(UNROLL):
                    totals(i * UNROLL + (u + 1))
            totals(BITS + 1)
            for k, flags in ((1, tied), (2, picked)):
                pe.wait_ge(pre_in, k)
                nc.tensor.matmul(ps_a[:, 0, 0:SC], before[:, :], flags[:, :, :].rearrange("p e t -> p (e t)"), start=True, stop=True)
                nc.tensor.matmul(ps_a[:, 1, 0:SC], ones[:, :], flags[:, :, :].rearrange("p e t -> p (e t)"),
                                 start=True, stop=True).then_inc(pre_out, 1)

            def list_ids(e, q):
                pe.wait_ge(hot_ready, e + 1)
                pe.wait_ge(id_free, e + 1)
                for t in range(NT):
                    last = nc.tensor.matmul(ps_a[0:HI, 0, 0:2 * LO], hot_hi[:, q, t, :], hot_id[:, q, t, :, :].rearrange("p a b -> p (a b)"),
                                            start=(t == 0), stop=(t == NT - 1))
                last.then_inc(id_sum, 1)

            def turn_tokens(e, q):
                pe.wait_ge(gathered, e * (16 * CT) + 16 * CT)
                for k in range(KT):
                    pe.wait_ge(t_free, e * KT + (k + 1))
                    if k == 0:
                        pe.wait_ge(id_free, e + 2)
                    for c in range(CT):
                        last = nc.tensor.transpose(ps_a[:, k, c * P:(c + 1) * P], tok[:, q, c, k * P:(k + 1) * P], ident[:, :])
                    last.then_inc(t_ready, 1)

            def hidden(e, q, ft):
                pe.wait_ge(relu_done, e * FT + (ft + 1))
                n = 0
                for k in range(KT):
                    for wp, xp in ((0, tok_h), (0, tok_l), (1, tok_h)):
                        last = nc.tensor.matmul(ps_h[:, ft % 2, :], w1[:, q, wp, k, ft * P:(ft + 1) * P], xp[:, q, k, :],
                                                start=(n == 0), stop=(n == 3 * KT - 1))
                        n += 1
                last.then_inc(g_ready, 1)

            def result(e, q, ft):
                pe.wait_ge(hid_low, e * FT + (ft + 3))
                if ft == 0:
                    pe.wait_ge(y_free, e + 1)
                for c in range(CT):
                    at = slice(c * P, (c + 1) * P)
                    for n, (xp, wp) in enumerate(((hid_h, 0), (hid_h, 1), (hid_l, 0))):
                        last = nc.tensor.matmul(ps_y[:, c, 0:C], xp[:, ft % 4, at], w2[:, q, wp, ft, :],
                                                start=(ft == 0 and n == 0), stop=(ft == FT - 1 and n == 2))
                last.then_inc(y_ready, 1)

            def expert(e, q, nxt):
                pe.wait_ge(w1_low, e + 1)
                pe.wait_ge(w2_low, e * 2 + 2)
                pe.wait_ge(t_free, e * KT + (2 + KT))
                for ft in range(FT):
                    hidden(e, q, ft)
                    if ft >= 2:
                        result(e, q, ft - 2)
                    if nxt and ft == 3:
                        list_ids(e + 1, 1 - q)
                    if nxt and ft == FT - 1:
                        turn_tokens(e + 1, 1 - q)
                result(e, q, FT - 2)
                result(e, q, FT - 1)

            list_ids(0, 0)
            turn_tokens(0, 0)
            with pe.Fori(0, E_N // 2 - 1) as i:
                for q in range(2):
                    expert(i * 2 + q, q, True)
            expert(E_N - 2, 0, True)
            expert(E_N - 1, 1, False)

        @block.scalar
        def _(act):
            act.sem_inc(relu_done, 2)
            def high_w(e, q, part):
                if part == 0:
                    act.wait_ge(w_loaded[q], e * 16 + (32 - 16 * q))
                if part < 2:
                    nc.scalar.activation(w1[:, q, 0, part, :], w1r[:, q, part, :], ACT.Copy).then_inc(w_high, 1)
                else:
                    at = slice((part - 2) * FT // 2, (part - 1) * FT // 2)
                    nc.scalar.activation(w2[:, q, 0, at, :], w2r[:, q, at, :], ACT.Copy).then_inc(w_high, 1)

            act.wait_ge(exp_in, 1)
            nc.scalar.activation(logits[:, :, :], logits[:, :, :], ACT.Exp).then_inc(exp_out, 1)
            for part in range(4):
                high_w(0, 0, part)

            def high_tokens(e, q):
                for k in range(KT):
                    act.wait_ge(t_ready, e * KT + (k + 1))
                    nc.scalar.activation(tok_h[:, q, k, :], ps_a[:, k, :], ACT.Copy).then_inc(t_high, 1)

            def expert(e, q, nxt):
                for ft in range(FT):
                    act.wait_ge(g_ready, e * FT + (ft + 1))
                    act.wait_ge(hid_low, e * FT + (ft + 1))
                    nc.scalar.activation(relu[:, ft % 2, :], ps_h[:, ft % 2, :], ACT.Relu,
                                         bias=b1[:, e, ft:ft + 1]).then_inc(relu_done, 1)
                    if nxt and ft == 2:
                        act.wait_ge(y_ready, e * FT + 1)
                    if nxt and 2 <= ft <= 5:
                        high_w(e + 1, 1 - q, ft - 2)
                    if nxt and ft == FT - 1:
                        high_tokens(e + 1, 1 - q)

            act.wait_ge(in_loaded, 32)
            high_tokens(0, 0)
            with act.Fori(0, E_N // 2 - 1) as i:
                for q in range(2):
                    expert(i * 2 + q, q, True)
            expert(E_N - 2, 0, True)
            expert(E_N - 1, 1, False)

        @block.vector
        def _(dve):
            dve.sem_inc(t_free, 2)
            dve.sem_inc(id_free, 1)
            dve.sem_inc(y_free, 1)
            dve.sem_inc(hid_low, 2)
            n = [0]

            def link(ins):
                n[0] += 1
                ins.then_inc(dve_chain, 1)
                dve.wait_ge(dve_chain, n[0])


            link(nc.vector.tensor_reduce(top[:, :], logits[:, :, :], AX.X, ALU.max))
            nc.vector.tensor_tensor(out=logits[:, :, :], in0=logits[:, :, :], in1=top[:, :].unsqueeze(2).to_broadcast([P, NT, E_N]),
                                    op=ALU.subtract).then_inc(exp_in, 1)
            dve.wait_ge(exp_out, 1)
            link(nc.vector.tensor_reduce(tot[:, :], logits[:, :, :], AX.X, ALU.add))
            link(nc.vector.reciprocal(tot[:, :], tot[:, :]))
            nc.vector.tensor_tensor(out=logits[:, :, :], in0=logits[:, :, :], in1=tot[:, :].unsqueeze(2).to_broadcast([P, NT, E_N]),
                                    op=ALU.mult).then_inc(scored, 1)
            dve.wait_ge(scored, 1)
            dve.wait_ge(consts, 1)
            nc.vector.memset(bit[:, 0, :], 1 << (BITS - 1))
            nc.vector.memset(cand[:, :], 1 << (BITS - 1))
            link(nc.vector.tensor_copy(score[:, :, :], logits[:, :, :].rearrange("p t e -> p e t")))

            STEPS = 5
            base = n[0]

            def bit_step(k, q, chain):
                done = 0

                def after(ins):
                    nonlocal done
                    done += 1
                    ins.then_inc(dve_chain, 1)
                    dve.wait_ge(dve_chain, chain + done)

                after(nc.vector.tensor_tensor(out=ge[:, :, :], in0=score[:, :, :],
                                              in1=cand[:, :].bitcast(F32).unsqueeze(2).to_broadcast([P, E_N, NT]), op=ALU.is_ge))
                with nc.allow_low_precision("counts up to 32 are exact"):
                    nc.vector.tensor_reduce(cnt[:, :], ge[:, :, :], AX.X, ALU.add).then_inc(cnt_ready, 1)
                nc.vector.tensor_scalar(out=bit[:, 1 - q, :], in0=bit[:, q, :], scalar1=1, scalar2=None,
                                        op0=ALU.logical_shift_right)
                nc.vector.tensor_tensor(out=thr[:, :], in0=cand[:, :], in1=bit[:, q, :], op=ALU.bitwise_xor).then_inc(dve_chain, 1)
                done += 1
                dve.wait_ge(dve_chain, chain + done)
                nc.vector.tensor_tensor(out=thr[:, :], in0=thr[:, :], in1=bit[:, 1 - q, :], op=ALU.bitwise_or).then_inc(dve_chain, 1)
                done += 1
                dve.wait_ge(cnt_sum, k)
                after(nc.vector.scalar_tensor_tensor(out=won[:, :], in0=ps_h[:, 0, 0:E_N], scalar=float(CAP), in1=bit[:, q, :],
                                                     op0=ALU.is_ge, op1=ALU.mult))
                after(nc.vector.tensor_tensor(out=cand[:, :], in0=thr[:, :], in1=won[:, :], op=ALU.bitwise_or))
                assert done == STEPS

            with dve.Fori(0, BITS // UNROLL) as i:
                for u in range(UNROLL):
                    bit_step(i * UNROLL + (u + 1), u % 2, i * (STEPS * UNROLL) + (base + STEPS * u))
            n[0] = base + BITS * STEPS

            def at_thr():
                return cand[:, :].bitcast(F32).unsqueeze(2).to_broadcast([P, E_N, NT])

            link(nc.vector.tensor_tensor(out=above[:, :, :], in0=score[:, :, :], in1=at_thr(), op=ALU.is_gt))
            nc.vector.tensor_tensor(out=tied[:, :, :], in0=score[:, :, :], in1=at_thr(), op=ALU.is_equal).then_inc(pre_in, 1)
            with nc.allow_low_precision("counts up to 32 are exact"):
                nc.vector.tensor_reduce(cnt[:, :], above[:, :, :], AX.X, ALU.add).then_inc(cnt_ready, 1)
            dve.wait_ge(cnt_sum, BITS + 1)
            link(nc.vector.tensor_scalar(out=need[:, :], in0=ps_h[:, 0, 0:E_N], scalar1=-1.0, scalar2=float(CAP), op0=ALU.mult, op1=ALU.add))

            def ranks(k):
                dve.wait_ge(pre_out, k)
                link(nc.vector.tensor_tensor_scan(out=scan[:, :], data0=restart[:, :, :].rearrange("p e t -> p (e t)"),
                                                  data1=ps_a[:, 1, 0:SC], initial=0.0, op0=ALU.mult, op1=ALU.add))
                link(nc.vector.tensor_tensor(out=scan[:, :], in0=scan[:, :], in1=ps_a[:, 1, 0:SC], op=ALU.subtract))
                link(nc.vector.tensor_tensor(out=rank[:, :], in0=scan[:, :], in1=ps_a[:, 0, 0:SC], op=ALU.add))

            rank_v = rank[:, :].rearrange("p (e t) -> p e t", e=E_N)
            ranks(1)
            link(nc.vector.tensor_tensor(out=rank_v, in0=rank_v, in1=need[:, :].unsqueeze(2).to_broadcast([P, E_N, NT]), op=ALU.is_lt))
            link(nc.vector.tensor_tensor(out=rank_v, in0=rank_v, in1=tied[:, :, :], op=ALU.mult))
            nc.vector.tensor_tensor(out=picked[:, :, :], in0=rank_v, in1=above[:, :, :], op=ALU.add).then_inc(pre_in, 1)
            dve.wait_ge(pre_in, 2)
            ranks(2)
            link(nc.vector.scalar_tensor_tensor(out=rank_v, in0=rank_v, scalar=1.0, in1=picked[:, :, :], op0=ALU.add, op1=ALU.mult))
            link(nc.vector.tensor_scalar(out=place[:, :, :], in0=rank_v, scalar1=-1.0, scalar2=None, op0=ALU.add))
            link(nc.vector.tensor_scalar(out=place_hi[:, :, :], in0=place[:, :, :], scalar1=4, scalar2=None, op0=ALU.arith_shift_right))
            link(nc.vector.tensor_scalar(out=place_lo[:, :, :], in0=place[:, :, :], scalar1=LO - 1, scalar2=None, op0=ALU.bitwise_and))
            HOTS = 1
            IDS = 1

            def one_hots(e, q, chain):
                hi, lo = (v[:, e, :].unsqueeze(2) for v in (place_hi, place_lo))
                nc.vector.tensor_tensor(out=hot_hi[:, q, :, :], in0=hi.to_broadcast([P, NT, HI]),
                                        in1=iota[:, :].unsqueeze(1).to_broadcast([P, NT, HI]), op=ALU.is_equal)
                nc.vector.tensor_tensor(out=hot_lo[:, q, :, :], in0=lo.to_broadcast([P, NT, LO]),
                                        in1=iota[:, 0:LO].unsqueeze(1).to_broadcast([P, NT, LO]), op=ALU.is_equal).then_inc(dve_chain, 1)
                dve.wait_ge(dve_chain, chain + 1)
                nc.vector.tensor_tensor(out=hot_id[:, q, :, 0, :], in0=hot_lo[:, q, :, :],
                                        in1=tile_no[:, :].unsqueeze(2).to_broadcast([P, NT, LO]), op=ALU.mult)
                nc.vector.tensor_scalar(out=hot_id[:, q, :, 1, :], in0=hot_lo[:, q, :, :], scalar1=part_no[:, 0:1], scalar2=None,
                                        op0=ALU.mult).then_inc(hot_ready, 1)

            def take_ids(e, q, chain):
                dve.wait_ge(id_sum, e + 1)
                nc.vector.tensor_copy(id_part[:, q, :], ps_a[0:HI, 0, LO:2 * LO]).then_inc(dve_chain, 1)
                dve.wait_ge(dve_chain, chain + 1)
                dve.sem_inc(held, 1)
                nc.vector.scalar_tensor_tensor(out=id_tok[:, q, :], in0=ps_a[0:HI, 0, 0:LO], scalar=float(P), in1=id_part[:, q, :],
                                               op0=ALU.mult, op1=ALU.add).then_inc(id_ready, 1)
                dve.wait_ge(id_ready, e + 1)
                dve.sem_inc(id_free, 1)

            def low_w2(e, q, part):
                at = slice(part * FT // 2, (part + 1) * FT // 2)
                dve.wait_ge(w_high, e * 4 + (part + 3))
                nc.vector.tensor_tensor(out=w2[:, q, 1, at, :], in0=w2r[:, q, at, :], in1=w2[:, q, 0, at, :].bitcast(F32),
                                        op=ALU.subtract).then_inc(w2_low, 1)

            def low_tokens(e, q):
                for k in range(KT):
                    dve.wait_ge(t_high, e * KT + (k + 1))
                    nc.vector.tensor_tensor(out=tok_l[:, q, k, :], in0=ps_a[:, k, :], in1=tok_h[:, q, k, :].bitcast(F32),
                                            op=ALU.subtract).then_inc(t_free, 1)

            PER = HOTS + IDS
            e_base = n[0]
            dve.wait_ge(in_loaded, 32)
            one_hots(0, 0, e_base)
            low_w2(0, 0, 0)
            low_w2(0, 0, 1)
            take_ids(0, 0, e_base + 1)
            low_tokens(0, 0)
            e_base += PER

            def expert(e, q, nxt, chain):
                for ft in range(FT):
                    dve.wait_ge(relu_done, e * FT + (ft + 3))
                    nc.vector.tensor_copy(hid_h[:, ft % 4, :], relu[:, ft % 2, :]).then_inc(hid_high, 1)
                    dve.wait_ge(hid_high, e * FT + (ft + 1))
                    nc.vector.tensor_tensor(out=hid_l[:, ft % 4, :], in0=relu[:, ft % 2, :], in1=hid_h[:, ft % 4, :].bitcast(F32),
                                            op=ALU.subtract).then_inc(hid_low, 1)
                    if nxt and ft == 0:
                        one_hots(e + 1, 1 - q, chain)
                    if nxt and ft == 3:
                        take_ids(e + 1, 1 - q, chain + 1)
                    if nxt and 5 <= ft <= 6:
                        low_w2(e + 1, 1 - q, ft - 5)
                    if nxt and ft == FT - 1:
                        low_tokens(e + 1, 1 - q)
                dve.wait_ge(y_ready, e * FT + FT)
                dve.wait_ge(part_free, e + 1)
                for c in range(CT):
                    last = nc.vector.tensor_tensor(out=part[:, c, :], in0=ps_y[:, c, 0:C], in1=b2[:, e, :], op=ALU.add)
                last.then_inc(y_free, 1)
                dve.wait_ge(y_free, e + 2)
                dve.sem_inc(held, 1)
                for c in range(CT):
                    nc.vector.tensor_scalar(out=part[:, c, :], in0=part[:, c, :], scalar1=tok[:, q, c, bass.ds(C + e, 1)],
                                            scalar2=None, op0=ALU.mult).then_inc(weighted, 1)

            with dve.Fori(0, E_N // 2 - 1) as i:
                for q in range(2):
                    expert(i * 2 + q, q, True, i * (2 * PER) + (e_base + q * PER))
            expert(E_N - 2, 0, True, (E_N - 2) * PER + e_base)
            expert(E_N - 1, 1, False, 0)


def layout(inputs):
    import numpy as np

    def arr(k):
        return np.asarray(inputs[k])

    def stack_order(w):
        v = w.reshape(w.shape[:-1] + (2, 8, 2, 8))
        n = v.ndim
        return v.transpose(tuple(range(n - 4)) + (n - 2, n - 4, n - 1, n - 3)).reshape(w.shape)

    out = {
        "x": arr("x").reshape(NTOK, C),
        "down_t": np.stack([arr(f"L0_attn_W{k}_down").T for k in "qkv"]),
        "wc": arr("L0_attn_Wc"),
        "q_c": arr("L0_attn_Wq_up_c"), "q_e": arr("L0_attn_Wq_up_e"),
        "k_c": arr("L0_attn_Wk_up_c"), "k_e": arr("L0_attn_Wk_up_e"),
        "v_up": arr("L0_attn_Wv_up"),
        "ctx_t": arr("ctx_1024").transpose(0, 2, 1),
        "mask": arr("mask_1x1xSxS2_bk0")[0, 0],
        "mask_t": arr("mask_1x1xSxS2_bk0")[0, 0].T.copy(),
        "w_q": stack_order(arr("L0_xattn_w_q").T), "w_k": stack_order(arr("L0_xattn_w_k").T),
        "w_v": arr("L0_xattn_w_v").T, "w_o": arr("L0_xattn_w_o").T,
        "b_qk": np.stack([stack_order(arr(f"L0_xattn_b_{k}")).reshape(2, P).T for k in "qk"], axis=1),
        "b_v": arr("L0_xattn_b_v"), "b_o": arr("L0_xattn_b_o"),
        "router_w": arr("L0_ffn_router_w"), "router_b": arr("L0_ffn_router_b"),
        "w1": arr("L0_ffn_w1"), "b1": arr("L0_ffn_b1").reshape(E_N, DFF // P, P).transpose(2, 0, 1), "w2": arr("L0_ffn_w2"), "b2": arr("L0_ffn_b2"),
    }
    dim = DH // 2
    inv = (1.0 / 10000.0 ** (np.arange(0, dim, 2, dtype=np.float32) / np.float32(dim))).astype(np.float32)
    ang = np.arange(S, dtype=np.float32)[None, :] * np.concatenate((inv, inv))[:, None]
    sign = np.where(np.arange(dim) % 2 == 0, -1.0, 1.0).astype(np.float32)[:, None]
    rows = (np.arange(P) // 8) % 8
    out["cos"] = np.cos(ang).astype(np.float32)[rows]
    out["sin"] = (np.sin(ang).astype(np.float32) * sign)[rows]
    return {k: np.ascontiguousarray(v) for k, v in out.items()}


def decoder_layer(nc, dram, out, what="all"):
    with ExitStack() as ctx:
        ident = ctx.enter_context(nc.sbuf_tensor("ident", [P, P], F32))
        identb = ctx.enter_context(nc.sbuf_tensor("identb", [P, P], BF16))
        made = ctx.enter_context(nc.semaphore("ident_made"))
        with nc.Block() as block:
            @block.gpsimd
            def _(pool):
                nc.gpsimd.memset(ident[:, :], 0.0).then_inc(made, 1)
                nc.gpsimd.memset(identb[:, :], 0.0).then_inc(made, 1)
                pool.wait_ge(made, 2)
                for t in (ident, identb):
                    nc.gpsimd.affine_select(out=t[:, :], in_=t[:, :], compare_op=ALU.not_equal, fill=1.0, base=0,
                                            pattern=[[-1, P]], channel_multiplier=1).then_inc(made, 1)
                pool.wait_ge(made, 4)
        x1 = nc.dram_tensor("x_after_self", [NTOK, C], F32).ap()
        table = nc.dram_tensor("rows_with_scores", [NTOK, ROW], F32).ap()
        logits = ctx.enter_context(nc.sbuf_tensor("logits", [P, NT, E_N], F32))
        with ExitStack() as layers:
            qst = layers.enter_context(nc.sbuf_tensor("qst", [P, 2, 8, S], F32R))
            kst = layers.enter_context(nc.sbuf_tensor("kst", [P, 2, 8, S], F32R))
            vals = layers.enter_context(nc.sbuf_tensor("vals", [P, TT, H, 32], F32))
            shared = (qst, kst, vals)
            attention_layer(nc, False, dram["x"], out if what == "self" else x1, dram, ident, identb, shared)
            if what == "self":
                return
            attention_layer(nc, True, x1, out, dram, ident, identb, shared, table, logits)
        if what == "all":
            mixture(nc, out, table, logits, dram, ident)


def kernel(**inputs):
    import numpy as np
    import concourse.bacc as bacc
    from concourse.bass_utils import run_bass_kernel_spmd

    nc = bacc.Bacc("TRN2", target_bir_lowering=False, num_devices=1)
    arrays, dram = {}, {}
    for name, a in layout(inputs).items():
        arrays[f"in_{name}_dram"] = a
        dram[name] = nc.dram_tensor(f"in_{name}_dram", a.shape, mybir.dt.from_np(a.dtype), kind="ExternalInput").ap()
    out = nc.dram_tensor("out_dram", [NTOK, C], F32, kind="ExternalOutput").ap()
    decoder_layer(nc, dram, out)
    got = run_bass_kernel_spmd(nc, [arrays], core_ids=[0])
    return np.asarray(got.results[0]["out_dram"]).reshape(B, S, C)
```
